# Optimizing a Trainium2 kernel written in Bass

```python
import numpy as np
import jax
import jax.numpy as jnp

def _softmax(x, axis=-1):
    return jax.nn.softmax(x, axis=axis)

def _gelu(x):
    return jax.nn.gelu(x, approximate=True)

def _silu(x):
    return jax.nn.silu(x)

def _sigmoid(x):
    return jax.nn.sigmoid(x)

def _layernorm(x, axis=-1, eps=1e-05):
    m = jnp.mean(x, axis=axis, keepdims=True)
    v = jnp.var(x, axis=axis, keepdims=True)
    return (x - m) / jnp.sqrt(v + eps)

def _scatter_add(tgt, idx, src, axis=0):
    return tgt.at[idx].add(src)

def _segment_sum(src, seg, n):
    return jax.ops.segment_sum(src, seg, n)
kernel_name = 'mk_seq_postln_d2_jaxref_r8_47fc44'

def setup_inputs(seed: int=0):
    np.random.seed(seed)
    _w = jnp.asarray

    def _L0_attn_setup():
        import jax, jax.numpy as jnp
        import numpy as np
        import math
        H = 16
        DN = 128
        DR = 64
        DV = 128
        ROPE_BASE = 10000.0

        def _rope_cos_sin(seq_len, dim, dtype):
            inv_freq = 1.0 / ROPE_BASE ** (jnp.arange(0, dim, 2, dtype=jnp.float32) / dim)
            t = jnp.arange(seq_len, dtype=jnp.float32)
            freqs = t[:, None] * inv_freq[None, :]
            return (jnp.cos(freqs).astype(dtype), jnp.sin(freqs).astype(dtype))

        def _apply_rope(x, cos, sin):
            half = x.shape[-1] // 2
            x1, x2 = (x[..., :half], x[..., half:])
            c = cos[None, :, None, :]
            s = sin[None, :, None, :]
            return jnp.concatenate([x1 * c - x2 * s, x1 * s + x2 * c], axis=-1)
        key = jax.random.key(seed)
        ks = jax.random.split(key, 5)
        hidden = 256
        B, S = (1, 256)
        q_size = H * (DN + DR)
        v_size = H * DV
        std = 0.02
        return {'hidden_states': jax.random.normal(ks[0], (B, S, hidden), jnp.float32), 'Wq': jax.random.normal(ks[1], (q_size, hidden), jnp.float32) * std, 'Wk': jax.random.normal(ks[2], (q_size, hidden), jnp.float32) * std, 'Wv': jax.random.normal(ks[3], (v_size, hidden), jnp.float32) * std, 'Wo': jax.random.normal(ks[4], (hidden, v_size), jnp.float32) * std}
    _L0_attn_in = _L0_attn_setup()

    def _L0_ffn_setup():
        import jax, jax.numpy as jnp
        import numpy as np
        B, S, D, H = (4, 256, 256, 1024)

        def fwht(x):
            orig_shape = x.shape
            n = orig_shape[-1]
            x = x.reshape(-1, n)
            h = 1
            while h < n:
                xb = x.reshape(-1, n // (2 * h), 2, h)
                a = xb[:, :, 0, :]
                b = xb[:, :, 1, :]
                x = jnp.stack([a + b, a - b], axis=2).reshape(-1, n)
                h *= 2
            scale = jnp.asarray(1.0 / np.sqrt(n), dtype=x.dtype)
            return (x * scale).reshape(orig_shape)
        key = jax.random.key(seed)
        kx, k1, k2, k3 = jax.random.split(key, 4)
        x = jax.random.normal(kx, (B, S, D), dtype=jnp.float32)
        W1 = jax.random.normal(k1, (H, D), dtype=jnp.float32) * (1.0 / np.sqrt(D))
        W2 = jax.random.normal(k2, (D, H), dtype=jnp.float32) * (1.0 / np.sqrt(H))
        W3 = jax.random.normal(k3, (H, D), dtype=jnp.float32) * (1.0 / np.sqrt(D))
        return {'x': x, 'W1': W1, 'W2': W2, 'W3': W3}
    _L0_ffn_in = _L0_ffn_setup()

    def _L1_attn_setup():
        import jax, jax.numpy as jnp
        import numpy as np
        D = 256
        H = 8
        QK = D // 2
        FF = 1024
        CAP = 15.0
        EPS = 1e-06

        def _rmsnorm(x, w, eps=EPS):
            xf = x.astype(jnp.float32)
            var = jnp.mean(xf * xf, axis=-1, keepdims=True)
            return (w * xf * jax.lax.rsqrt(var + eps)).astype(x.dtype)

        def _soft_cap(x, cap=CAP):
            return cap * jnp.tanh(x / cap)

        def _mlstm_parallel(q, k, v, i_pre, f_pre):
            B, Hn, S, dqk = q.shape
            logfg = jax.nn.log_sigmoid(f_pre)
            Fcum = jnp.cumsum(logfg, axis=-1)
            Dmat = Fcum[..., :, None] - Fcum[..., None, :] + i_pre[..., None, :]
            causal = jnp.tril(jnp.ones((S, S), dtype=bool))
            Dmat = jnp.where(causal, Dmat, -jnp.inf)
            m = jnp.max(Dmat, axis=-1, keepdims=True)
            Smat = jnp.exp(Dmat - m)
            qk = jnp.einsum('bhsd,bhtd->bhst', q, k) / jnp.sqrt(jnp.float32(dqk))
            C = qk * Smat
            n = jnp.maximum(jnp.abs(jnp.sum(C, axis=-1, keepdims=True)), jnp.exp(-m))
            h = jnp.einsum('bhst,bhtd->bhsd', C / n, v)
            return h
        key = jax.random.key(seed)
        ks = jax.random.split(key, 17)
        sc = 0.02
        inp = {'x': jax.random.normal(ks[0], (2, 256, D), jnp.float32), 'norm1_w': jnp.ones((D,), jnp.float32), 'wq': jax.random.normal(ks[1], (D, QK), jnp.float32) * sc, 'wk': jax.random.normal(ks[2], (D, QK), jnp.float32) * sc, 'wv': jax.random.normal(ks[3], (D, D), jnp.float32) * sc, 'w_ig': jax.random.normal(ks[4], (D, H), jnp.float32) * sc, 'b_ig': jnp.zeros((H,), jnp.float32), 'w_fg': jax.random.normal(ks[5], (D, H), jnp.float32) * sc, 'b_fg': jnp.linspace(3.0, 6.0, H).astype(jnp.float32), 'w_og': jax.random.normal(ks[6], (D, D), jnp.float32) * sc, 'mh_w': jnp.ones((D,), jnp.float32), 'w_out': jax.random.normal(ks[7], (D, D), jnp.float32) * sc, 'norm2_w': jnp.ones((D,), jnp.float32), 'w_gate': jax.random.normal(ks[8], (D, FF), jnp.float32) * sc, 'w_up': jax.random.normal(ks[9], (D, FF), jnp.float32) * sc, 'w_down': jax.random.normal(ks[10], (FF, D), jnp.float32) * sc}
        return inp
    _L1_attn_in = _L1_attn_setup()

    def _L1_ffn_setup():
        import jax, jax.numpy as jnp
        import numpy as np
        HIDDEN = 256
        INTER = 1024
        B, S = (4, 128)

        def _qmatmul(x, w_int8, scale):
            y = jnp.einsum('bsh,ho->bso', x, w_int8.astype(x.dtype))
            return y * scale
        key = jax.random.key(seed)
        ks = jax.random.split(key, 7)
        x = jax.random.normal(ks[0], (B, S, HIDDEN), dtype=jnp.float32)
        w_gate = jax.random.randint(ks[1], (HIDDEN, INTER), -128, 128, dtype=jnp.int32).astype(jnp.int8)
        w_up = jax.random.randint(ks[2], (HIDDEN, INTER), -128, 128, dtype=jnp.int32).astype(jnp.int8)
        w_down = jax.random.randint(ks[3], (INTER, HIDDEN), -128, 128, dtype=jnp.int32).astype(jnp.int8)
        s_gate = jax.random.uniform(ks[4], (INTER,), dtype=jnp.float32) * 0.02 + 0.001
        s_up = jax.random.uniform(ks[5], (INTER,), dtype=jnp.float32) * 0.02 + 0.001
        s_down = jax.random.uniform(ks[6], (HIDDEN,), dtype=jnp.float32) * 0.02 + 0.001
        return {'x': x, 'w_gate': w_gate, 'w_up': w_up, 'w_down': w_down, 's_gate': s_gate, 's_up': s_up, 's_down': s_down}
    _L1_ffn_in = _L1_ffn_setup()
    _d = {'L0_attn_hidden_states': _L0_attn_in['hidden_states'], 'L0_attn_Wq': _L0_attn_in['Wq'], 'L0_attn_Wk': _L0_attn_in['Wk'], 'L0_attn_Wv': _L0_attn_in['Wv'], 'L0_attn_Wo': _L0_attn_in['Wo'], 'L0_ffn_W1': _L0_ffn_in['W1'], 'L0_ffn_W2': _L0_ffn_in['W2'], 'L0_ffn_W3': _L0_ffn_in['W3'], 'L1_attn_norm1_w': _L1_attn_in['norm1_w'], 'L1_attn_wq': _L1_attn_in['wq'], 'L1_attn_wk': _L1_attn_in['wk'], 'L1_attn_wv': _L1_attn_in['wv'], 'L1_attn_w_ig': _L1_attn_in['w_ig'], 'L1_attn_b_ig': _L1_attn_in['b_ig'], 'L1_attn_w_fg': _L1_attn_in['w_fg'], 'L1_attn_b_fg': _L1_attn_in['b_fg'], 'L1_attn_w_og': _L1_attn_in['w_og'], 'L1_attn_mh_w': _L1_attn_in['mh_w'], 'L1_attn_w_out': _L1_attn_in['w_out'], 'L1_attn_norm2_w': _L1_attn_in['norm2_w'], 'L1_attn_w_gate': _L1_attn_in['w_gate'], 'L1_attn_w_up': _L1_attn_in['w_up'], 'L1_attn_w_down': _L1_attn_in['w_down'], 'L1_ffn_w_gate': _L1_ffn_in['w_gate'], 'L1_ffn_w_up': _L1_ffn_in['w_up'], 'L1_ffn_w_down': _L1_ffn_in['w_down'], 'L1_ffn_s_gate': _L1_ffn_in['s_gate'], 'L1_ffn_s_up': _L1_ffn_in['s_up'], 'L1_ffn_s_down': _L1_ffn_in['s_down']}
    _x0 = _d['L0_attn_hidden_states']
    _d['L0_attn_hidden_states'] = jax.random.normal(jax.random.fold_in(jax.random.key(seed), 1), (4, 256, 256), dtype=_x0.dtype)
    del _x0
    return _d

def reference(L0_attn_hidden_states, L0_attn_Wq, L0_attn_Wk, L0_attn_Wv, L0_attn_Wo, L0_ffn_W1, L0_ffn_W2, L0_ffn_W3, L1_attn_norm1_w, L1_attn_wq, L1_attn_wk, L1_attn_wv, L1_attn_w_ig, L1_attn_b_ig, L1_attn_w_fg, L1_attn_b_fg, L1_attn_w_og, L1_attn_mh_w, L1_attn_w_out, L1_attn_norm2_w, L1_attn_w_gate, L1_attn_w_up, L1_attn_w_down, L1_ffn_w_gate, L1_ffn_w_up, L1_ffn_w_down, L1_ffn_s_gate, L1_ffn_s_up, L1_ffn_s_down):

    def _L0_attn_ref(hidden_states, Wq, Wk, Wv, Wo):
        import jax, jax.numpy as jnp
        import numpy as np
        import math
        H = 16
        DN = 128
        DR = 64
        DV = 128
        ROPE_BASE = 10000.0

        def _rope_cos_sin(seq_len, dim, dtype):
            inv_freq = 1.0 / ROPE_BASE ** (jnp.arange(0, dim, 2, dtype=jnp.float32) / dim)
            t = jnp.arange(seq_len, dtype=jnp.float32)
            freqs = t[:, None] * inv_freq[None, :]
            return (jnp.cos(freqs).astype(dtype), jnp.sin(freqs).astype(dtype))

        def _apply_rope(x, cos, sin):
            half = x.shape[-1] // 2
            x1, x2 = (x[..., :half], x[..., half:])
            c = cos[None, :, None, :]
            s = sin[None, :, None, :]
            return jnp.concatenate([x1 * c - x2 * s, x1 * s + x2 * c], axis=-1)
        B, S, _ = hidden_states.shape
        q = hidden_states @ Wq.T
        k = hidden_states @ Wk.T
        v = hidden_states @ Wv.T
        q_nope = q[:, :, :H * DN].reshape(B, S, H, DN)
        q_rope = q[:, :, H * DN:].reshape(B, S, H, DR)
        k_nope = k[:, :, :H * DN].reshape(B, S, H, DN)
        k_rope = k[:, :, H * DN:].reshape(B, S, H, DR)
        v = v.reshape(B, S, H, DV)
        cos, sin = _rope_cos_sin(S, DR, hidden_states.dtype)
        q_rope = _apply_rope(q_rope, cos, sin)
        k_rope = _apply_rope(k_rope, cos, sin)
        scores = jnp.einsum('bqhd,bkhd->bhqk', q_nope, k_nope) / math.sqrt(DN) + jnp.einsum('bqhd,bkhd->bhqk', q_rope, k_rope) / math.sqrt(DR)
        attn = jax.nn.softmax(scores, axis=-1)
        out = jnp.einsum('bhqk,bkhd->bqhd', attn, v)
        out = out.reshape(B, S, H * DV)
        return out @ Wo.T

    def _L0_ffn_ref(x, W1, W2, W3):
        import jax, jax.numpy as jnp
        import numpy as np
        B, S, D, H = (4, 256, 256, 1024)

        def fwht(x):
            orig_shape = x.shape
            n = orig_shape[-1]
            x = x.reshape(-1, n)
            h = 1
            while h < n:
                xb = x.reshape(-1, n // (2 * h), 2, h)
                a = xb[:, :, 0, :]
                b = xb[:, :, 1, :]
                x = jnp.stack([a + b, a - b], axis=2).reshape(-1, n)
                h *= 2
            scale = jnp.asarray(1.0 / np.sqrt(n), dtype=x.dtype)
            return (x * scale).reshape(orig_shape)
        up_gate = jnp.einsum('bsd,hd->bsh', x, W1)
        up_lin = jnp.einsum('bsd,hd->bsh', x, W3)
        hidden = jax.nn.silu(up_gate) * up_lin
        hidden = fwht(hidden)
        out = jnp.einsum('bsh,dh->bsd', hidden, W2)
        return out

    def _L1_attn_ref(x, norm1_w, wq, wk, wv, w_ig, b_ig, w_fg, b_fg, w_og, mh_w, w_out, norm2_w, w_gate, w_up, w_down):
        import jax, jax.numpy as jnp
        import numpy as np
        D = 256
        H = 8
        QK = D // 2
        FF = 1024
        CAP = 15.0
        EPS = 1e-06

        def _rmsnorm(x, w, eps=EPS):
            xf = x.astype(jnp.float32)
            var = jnp.mean(xf * xf, axis=-1, keepdims=True)
            return (w * xf * jax.lax.rsqrt(var + eps)).astype(x.dtype)

        def _soft_cap(x, cap=CAP):
            return cap * jnp.tanh(x / cap)

        def _mlstm_parallel(q, k, v, i_pre, f_pre):
            B, Hn, S, dqk = q.shape
            logfg = jax.nn.log_sigmoid(f_pre)
            Fcum = jnp.cumsum(logfg, axis=-1)
            Dmat = Fcum[..., :, None] - Fcum[..., None, :] + i_pre[..., None, :]
            causal = jnp.tril(jnp.ones((S, S), dtype=bool))
            Dmat = jnp.where(causal, Dmat, -jnp.inf)
            m = jnp.max(Dmat, axis=-1, keepdims=True)
            Smat = jnp.exp(Dmat - m)
            qk = jnp.einsum('bhsd,bhtd->bhst', q, k) / jnp.sqrt(jnp.float32(dqk))
            C = qk * Smat
            n = jnp.maximum(jnp.abs(jnp.sum(C, axis=-1, keepdims=True)), jnp.exp(-m))
            h = jnp.einsum('bhst,bhtd->bhsd', C / n, v)
            return h
        B, S, _ = x.shape
        dqk, dv = (QK // H, D // H)
        h_in = _rmsnorm(x, norm1_w)
        q = (h_in @ wq).reshape(B, S, H, dqk).transpose(0, 2, 1, 3)
        k = (h_in @ wk).reshape(B, S, H, dqk).transpose(0, 2, 1, 3)
        v = (h_in @ wv).reshape(B, S, H, dv).transpose(0, 2, 1, 3)
        o_pre = h_in @ w_og
        i_pre = _soft_cap(h_in @ w_ig + b_ig).transpose(0, 2, 1)
        f_pre = _soft_cap(h_in @ w_fg + b_fg).transpose(0, 2, 1)
        h = _mlstm_parallel(q, k, v, i_pre, f_pre)
        h = h.transpose(0, 2, 1, 3)
        hf = h.astype(jnp.float32)
        var = jnp.mean(hf * hf, axis=-1, keepdims=True)
        h_norm = hf * jax.lax.rsqrt(var + EPS) * mh_w.reshape(H, dv)
        h_norm = h_norm.reshape(B, S, D)
        h_out = jax.nn.sigmoid(o_pre) * h_norm
        x1 = x + h_out @ w_out
        h2 = _rmsnorm(x1, norm2_w)
        mlp = jax.nn.silu(h2 @ w_gate) * (h2 @ w_up) @ w_down
        return x1 + mlp

    def _L1_ffn_ref(x, w_gate, w_up, w_down, s_gate, s_up, s_down):
        import jax, jax.numpy as jnp
        import numpy as np
        HIDDEN = 256
        INTER = 1024
        B, S = (4, 128)

        def _qmatmul(x, w_int8, scale):
            y = jnp.einsum('bsh,ho->bso', x, w_int8.astype(x.dtype))
            return y * scale
        gate = jax.nn.silu(_qmatmul(x, w_gate, s_gate))
        up = _qmatmul(x, w_up, s_up)
        fuse = gate * up
        return _qmatmul(fuse, w_down, s_down)
    x = L0_attn_hidden_states
    x = _layernorm(x + _L0_attn_ref(x, L0_attn_Wq, L0_attn_Wk, L0_attn_Wv, L0_attn_Wo), axis=-1)
    x = _layernorm(x + _L0_ffn_ref(x, L0_ffn_W1, L0_ffn_W2, L0_ffn_W3), axis=-1)
    x = _layernorm(x + _L1_attn_ref(x, L1_attn_norm1_w, L1_attn_wq, L1_attn_wk, L1_attn_wv, L1_attn_w_ig, L1_attn_b_ig, L1_attn_w_fg, L1_attn_b_fg, L1_attn_w_og, L1_attn_mh_w, L1_attn_w_out, L1_attn_norm2_w, L1_attn_w_gate, L1_attn_w_up, L1_attn_w_down), axis=-1)
    x = _layernorm(x + _L1_ffn_ref(x, L1_ffn_w_gate, L1_ffn_w_up, L1_ffn_w_down, L1_ffn_s_gate, L1_ffn_s_up, L1_ffn_s_down), axis=-1)
    return x

_drawn_inputs = setup_inputs


def setup_inputs(seed=0):
    import zlib

    import numpy as np

    out = dict(_drawn_inputs(seed))
    spreads = {'L1_attn_norm1_w': (1.0, 0.2),
     'L1_attn_b_ig': (0.0, 0.8),
     'L1_attn_mh_w': (1.0, 0.6),
     'L1_attn_norm2_w': (1.0, 0.6)}
    factors = {'L0_attn_Wq': 8.0, 'L0_attn_Wk': 8.0, 'L1_attn_w_fg': 8.0, 'L1_attn_w_og': 3.001}
    for name, (base, spread) in spreads.items():
        noise = np.random.default_rng([zlib.crc32(name.encode()), seed]).standard_normal(out[name].shape)
        drawn = base * np.exp(spread * noise) if base else spread * noise
        out[name] = jnp.asarray(drawn.astype(out[name].dtype))
    for name, factor in factors.items():
        out[name] = (out[name] * factor).astype(out[name].dtype)
    return out
```

```python
import math

import numpy as np
import concourse.bass as bass
from concourse import mybir
from contextlib import ExitStack

F32 = mybir.dt.float32
F32R = mybir.dt.float32r
BF16 = mybir.dt.bfloat16
I8 = mybir.dt.int8
ACT = mybir.ActivationFunctionType
ALU = mybir.AluOpType
AX = mybir.AxisListType

P = 128
B, S, D = 4, 256, 256
TOK = B * S
KT = D // P
TT = S // P
H, DN, DR, DV = 16, 128, 64, 128
HG = 4
NG = H // HG
SLOTS = NG * B
PIECE = 512
GP = 10
RING = 5
FF = 1024
FT = FF // P
SCALE = 1.0 / math.sqrt(DN)
LN_EPS = 1e-5


def attention(nc, keep, x_tok, x_T, w_att, w_ffn0, w2_raw, rope, ident_d):
    xTh, xTl, WBh, WBl, xres, ident = (keep[k] for k in ("xTh", "xTl", "WBh", "WBl", "xres", "ident"))
    rope_f = keep["stage"][:, 0:4 * PIECE].rearrange("p (a n) -> p a n", n=PIECE)
    with ExitStack() as ctx:
        def sb(name, shape, dt):
            return ctx.enter_context(nc.sbuf_tensor(name, shape, dt))

        def pb(name, shape, dt=F32):
            return ctx.enter_context(nc.psum_tensor(name, shape, dt))

        def sem(name):
            return ctx.enter_context(nc.semaphore(name))

        Vh = sb("Vh", [P, 2, TT, PIECE], F32R)
        Vl = sb("Vl", [P, 2, TT, PIECE], F32R)
        Q2 = sb("Q2", [P, 2, HG, S], F32R)
        K2 = sb("K2", [P, 2, HG, S], F32R)
        K3 = sb("K3", [P, 2, HG, S], F32R)
        rot_h = sb("rot_h", [P, 2, 2, S], F32R)
        rot_l = sb("rot_l", [P, 2, 2, S], F32R)
        OTh = sb("OTh", [P, 2, HG, S], F32R)
        OTl = sb("OTl", [P, 2, HG, S], F32R)
        PTh = sb("PTh", [P, 2, TT, S], F32R)
        PTl = sb("PTl", [P, 2, TT, S], F32R)
        raw = sb("raw", [P, RING, PIECE], F32)
        WOh, WOl = sb("WOh", [P, 2, PIECE], F32R), sb("WOl", [P, 2, PIECE], F32R)
        QKh = sb("QKh", [P, 2, HG, 2 * S], F32R)
        QKl = sb("QKl", [P, 2, HG, 2 * S], F32R)
        tables = sb("tables", [P, 2, 2, S], F32)
        probs = sb("probs", [P, 2, TT, S], F32)
        rmax = sb("rmax", [P, 2, TT], F32)
        nmax = sb("nmax", [P, 2, TT], F32)
        rsum = sb("rsum", [P, 2, TT], F32)
        rinv = sb("rinv", [P, 2, TT], F32)
        scr_q = nc.dram_tensor("scr_q", (2, 4, 32, HG, S), F32).ap()
        scr_k = nc.dram_tensor("scr_k", (2, 4, 32, HG, S), F32).ap()

        SC = [pb(f"SC{i}", [P, TT, S]) for i in range(2)]
        PT = pb("PT", [P, TT, S])
        O = pb("O", [P, 2 * S])
        PJ = [pb(f"PJ{i}", [P, 2 * S]) for i in range(3)]
        OUT = pb("OUT", [P, TT, D])
        BANK = [0, 1, 2, 0, 1, 2, 0, 1]

        x_in = sem("x_in")
        tab_in = sem("tab_in")
        res_in = sem("res_in")
        x_hi = sem("x_hi")
        x_split = sem("x_split")
        raw_in = [sem(f"raw_in{i}") for i in range(RING)]
        w_hi = sem("w_hi")
        w_split = sem("w_split")
        piece_ready = sem("piece_ready")
        part_hi = sem("part_hi")
        part_split = sem("part_split")
        rope_t = sem("rope_t")
        rope_prod = sem("rope_prod")
        rope_sum = sem("rope_sum")
        rope_hi = sem("rope_hi")
        rope_lo = sem("rope_lo")
        spill_q = sem("spill_q")
        spill_k = sem("spill_k")
        stack_q = sem("stack_q")
        stack_k = sem("stack_k")
        scores_ready = sem("scores_ready")
        rmax_ready = sem("rmax_ready")
        nmax_ready = sem("nmax_ready")
        exp_ready = sem("exp_ready")
        rinv_ready = sem("rinv_ready")
        probs_ready = sem("probs_ready")
        pT_ready = sem("pT_ready")
        pT_hi = sem("pT_hi")
        pT_split = sem("pT_split")
        head_ready = sem("head_ready")
        oT_hi = sem("oT_hi")
        oT_split = sem("oT_split")
        out_ready = sem("out_ready")
        acc_done = sem("acc_done")
        tiles_done = sem("tiles_done")


        def weights(i, hi):
            return (WBh if hi else WBl)[:, i, :] if i < 8 else (WOh if hi else WOl)[:, i - 8, :]

        block = ctx.enter_context(nc.Block())

        @block.sync
        def _(sp):
            sp.dma_start(rope_f[:, :, :].rearrange("p (t c) n -> p t c n", t=KT),
                         x_T.rearrange("(t p) (c n) -> p t c n", p=P, c=2)).then_inc(x_in, 16)
            for i in range(RING):
                sp.dma_start(raw[:, i, :], w_att[0, :, i, :]).then_inc(raw_in[i], 16)
            sp.dma_start(tables[:, :, :, :], rope).then_inc(tab_in, 16)
            sp.dma_start(ident[:, :], ident_d).then_inc(tab_in, 16)
            for i in range(RING):
                sp.wait_ge(w_split, i + 1)
                sp.dma_start(raw[:, i, :], w_att[0, :, RING + i, :]).then_inc(raw_in[i], 16)
            sp.dma_start(xres[:, :, :], x_tok.rearrange("(t p) d -> p t d", p=P)).then_inc(res_in, 16)

            def stacks(s, k):
                par = k % 2
                for i, (scr, spilled) in enumerate(((scr_q, spill_q), (scr_k, spill_k))):
                    for part, src, done in ((0, rot_h, rope_hi), (1, rot_l, rope_lo)):
                        sp.wait_ge(done, 2 * s + i + 1)
                        for half in range(2):
                            sp.dma_start(scr[par, 2 * part + half].rearrange("p j n -> j p n"),
                                         src[:, i, half, :].bitcast(F32)).then_inc(spilled, 16)
                sp.wait_ge(piece_ready, 8 * s + 2)
                sp.wait_ge(spill_q, 64 * (s + 1))
                sp.dma_start(Q2[:, par, :, :].bitcast(F32),
                             scr_q[par].rearrange("r p j n -> (r p) j n")).then_inc(stack_q, 16)
                sp.wait_ge(spill_k, 64 * (s + 1))
                for dst, r in ((K2, 0), (K3, 2)):
                    for half in range(2):
                        sp.dma_start(dst[64 * half:64 * half + 64, par, :, :].bitcast(F32),
                                     scr_k[par, r:r + 2].rearrange("r p j n -> (r p) j n")).then_inc(stack_k, 16)

            def emit(s, k):
                group_end = k % 4 == 2
                last_group = k == 14

                def load(i):
                    src = w_ffn0[:, i, :] if last_group else w_att_next(i)
                    sp.dma_start(raw[:, i % RING, :], src).then_inc(raw_in[i % RING], 16)

                def w_att_next(i):
                    return w_att[turn[0] + 1, :, i, :]

                pieces = FT if last_group else GP
                if group_end:
                    for i in range(RING):
                        sp.wait_ge(w_split, GP * (turn[0] + 1) - RING + i + 1)
                        sp.wait_ge(raw_in[i], 32)
                        load(i)
                if k < 15:
                    stacks(s + 1, k + 1)
                if group_end:
                    for i in range(RING, pieces):
                        sp.wait_ge(w_split, GP * (turn[0] + 1) + i - RING + 1)
                        sp.wait_ge(raw_in[i % RING], 48)
                        load(i)
                if k == 15:
                    for i in range(4):
                        sp.wait_ge(w_split, GP * NG + FT)
                        sp.dma_start(raw[:, i, :], w2_raw[:, i, :]).then_inc(raw_in[i], 16)

            stacks(0, 0)
            turn = [0]
            for s in (0, 1):
                emit(s, s)
            with sp.Fori(0, NG - 1) as g:
                turn[0] = g
                for k in range(2, 6):
                    emit(4 * g + k, k)
            turn[0] = NG - 1
            for s in (14, 15):
                emit(s, s)

        @block.tensor
        def _(pe):
            def three(out, lhs, rhs):
                n = len(lhs)
                for i, ((ah, al), (bh, bl)) in enumerate(zip(lhs, rhs)):
                    pe.matmul(out, ah, bh, start=(i == 0), stop=False)
                    pe.matmul(out, ah, bl, start=False, stop=False)
                    last = pe.matmul(out, al, bh, start=False, stop=(i == n - 1))
                return last

            def piece(s, k, p):
                b = k % 4
                out = PJ[BANK[p]]
                toks = slice(b * S, b * S + S)
                if k == 0:
                    if p == 0:
                        pe.wait_ge(x_split, 4)
                elif p < 3:
                    pe.wait_ge(part_split, 6 * s - [1, 0, 2][p])
                if p in (3, 4):
                    pe.wait_ge(rope_prod, 2 * s + p - 2)
                if p > 4:
                    pe.wait_ge(part_split, 6 * s + p - 4)
                if b == 0 and p % 2 == 0:
                    pe.wait_ge(w_split, GP * (s // 4 if isinstance(s, int) else group[0]) + 2 + p)
                if p < 2:
                    for c in range(2):
                        w = slice((2 * p + c) * P, (2 * p + c + 1) * P)
                        last = three(out[:, c * S:(c + 1) * S], [(WBh[:, t, w], WBl[:, t, w]) for t in range(KT)],
                                     [(xTh[:, t, toks], xTl[:, t, toks]) for t in range(KT)])
                elif p < 6:
                    j = p - 2
                    for c in range(2):
                        w = slice((2 * (j % 2) + c) * P, (2 * (j % 2) + c + 1) * P)
                        at = 2 + 2 * (j // 2)
                        last = three(out[:, c * S:(c + 1) * S], [(WBh[:, at + t, w], WBl[:, at + t, w]) for t in range(KT)],
                                     [(xTh[:, t, toks], xTl[:, t, toks]) for t in range(KT)])
                else:
                    rows = slice(b * S + (p - 6) * P, b * S + (p - 5) * P)
                    last = three(out[:, :], [(xTh[:, t, rows], xTl[:, t, rows]) for t in range(KT)],
                                 [(WBh[:, 6 + t, :], WBl[:, 6 + t, :]) for t in range(KT)])
                last.then_inc(piece_ready, 1)

            def scores(s, k, j):
                u, par, bank = 4 * s + j, k % 2, SC[j % 2]
                if j == 0:
                    pe.wait_ge(stack_q, 16 * (s + 1))
                    pe.wait_ge(stack_k, 64 * (s + 1))
                pe.wait_ge(part_split, 6 * s + j + 1)
                if k > 0 or j >= 2:
                    pe.wait_ge(exp_ready, u - 1)
                for t in range(TT):
                    q, keys = slice(t * P, (t + 1) * P), slice(S, 2 * S)
                    out = bank[:, t, :]
                    pe.matmul(out, QKh[:, par, j, q], QKh[:, par, j, keys], start=True, stop=False)
                    pe.matmul(out, QKh[:, par, j, q], QKl[:, par, j, keys], start=False, stop=False)
                    pe.matmul(out, QKl[:, par, j, q], QKh[:, par, j, keys], start=False, stop=False)
                    pe.matmul(out, Q2[:, par, j, q], K2[:, par, j, :], start=False, stop=False)
                    last = pe.matmul(out, Q2[:, par, j, q], K3[:, par, j, :], start=False, stop=True)
                last.then_inc(scores_ready, 1)

            def turn_probs(u, j, first):
                pe.wait_ge(probs_ready, u + 1)
                if not first:
                    pe.wait_ge(pT_split, u)
                for t in range(TT):
                    for c in range(TT):
                        last = pe.transpose(PT[:, c, t * P:(t + 1) * P], probs[:, j % 2, t, c * P:(c + 1) * P],
                                            ident[:, :])
                last.then_inc(pT_ready, 1)

            def values(u, s, k, j, first):
                if j == 0:
                    pe.wait_ge(part_split, 6 * s + 6)
                pe.wait_ge(pT_split, u + 1)
                if not first:
                    pe.wait_ge(oT_split, u)
                heads = slice(j * DV, (j + 1) * DV)
                last = three(O[:, 0:S], [(Vh[:, k % 2, t, heads], Vl[:, k % 2, t, heads]) for t in range(TT)],
                             [(PTh[:, j % 2, t, :], PTl[:, j % 2, t, :]) for t in range(TT)])
                last.then_inc(head_ready, 1)

            def output(s, k, first):
                if k % 4 == 0:
                    pe.wait_ge(w_split, GP * ((s // 4 if isinstance(s, int) else group[0]) + 1))
                pe.wait_ge(oT_split, 4 * s + 4)
                if not first:
                    pe.wait_ge(acc_done, s)
                for t in range(TT):
                    rows = slice(t * P, (t + 1) * P)
                    last = three(OUT[:, t, :], [(OTh[:, k % 2, j, rows], OTl[:, k % 2, j, rows]) for j in range(HG)],
                                 [(WOh[:, j // 2, (j % 2) * D:(j % 2 + 1) * D],
                                   WOl[:, j // 2, (j % 2) * D:(j % 2 + 1) * D]) for j in range(HG)])
                last.then_inc(out_ready, 1)

            BETWEEN = [([0, 1], [2]), ([3], [4]), ([5], [6]), ([7], [])]

            def emit(s, k):
                for j in range(HG):
                    u = 4 * s + j
                    scores(s, k, j)
                    if k < 15:
                        for p in BETWEEN[j][0]:
                            piece(s + 1, k + 1, p)
                    if k > 0 or j >= 1:
                        turn_probs(u - 1, (j - 1) % 4, first=(k == 0 and j == 1))
                    if k < 15:
                        for p in BETWEEN[j][1]:
                            piece(s + 1, k + 1, p)
                    if j == 3 and k > 0:
                        output(s - 1, k - 1, first=(k == 1))
                    if k > 0 or j >= 2:
                        back = (s, k) if j >= 2 else (s - 1, k - 1)
                        values(u - 2, *back, (j - 2) % 4, first=(k == 0 and j == 2))

            group = [0]
            for p in range(8):
                piece(0, 0, p)
            for s in (0, 1):
                emit(s, s)
            with pe.Fori(0, NG - 1) as g:
                group[0] = g + 1
                for k in range(2, 6):
                    emit(4 * g + k, k)
            for s in (14, 15):
                emit(s, s)
            last_u = 4 * SLOTS - 1
            turn_probs(last_u, 3, False)
            values(last_u - 1, SLOTS - 1, 15, 2, False)
            values(last_u, SLOTS - 1, 15, 3, False)
            output(SLOTS - 1, 15, False)

        ORDER = [([0, 1], [2]), ([3], [4]), ([5], [6]), ([7], [])]

        def part_dst(k, p, hi):
            if p < 6:
                return (QKh if hi else QKl)[:, k % 2, p - 2, :]
            return (Vh if hi else Vl)[:, k % 2, p - 6, :]

        @block.scalar
        def _(act):
            def part(s, k, p):
                if p < 2:
                    act.wait_ge(rope_sum, 4 * s + 2 * p + 2)
                    if k > 0:
                        act.wait_ge(spill_k if p else spill_q, 64 * s)
                    act.activation(rot_h[:, p, :, :], rope_f[:, 2 + p, :], ACT.Copy).then_inc(rope_hi, 1)
                else:
                    act.wait_ge(piece_ready, 8 * s + p + 1)
                    act.activation(part_dst(k, p, True), PJ[BANK[p]][:, :], ACT.Copy).then_inc(part_hi, 1)

            def exps(u, j):
                act.wait_ge(nmax_ready, u + 1)
                for t in range(TT):
                    last = act.activation(probs[:, j % 2, t, :], SC[j % 2][:, t, :], ACT.Exp, scale=SCALE,
                                          bias=nmax[:, j % 2, t:t + 1], accum_out=rsum[:, j % 2, t:t + 1])
                last.then_inc(exp_ready, 1)

            def pT(u, j):
                act.wait_ge(pT_ready, u + 1)
                act.activation(PTh[:, j % 2, :, :], PT[:, :, :], ACT.Copy).then_inc(pT_hi, 1)

            def oT(u, k, j):
                act.wait_ge(head_ready, u + 1)
                act.activation(OTh[:, k % 2, j, :], O[:, 0:S], ACT.Copy).then_inc(oT_hi, 1)

            def weight_piece(i, g, free):
                act.wait_ge(*free)
                act.wait_ge(raw_in[i % RING], 32 * g + 16 * (i // RING + 1))
                act.activation(weights(i, True), raw[:, i % RING, :], ACT.Copy).then_inc(w_hi, 1)

            REPLACED = [(), (0, 1), (2, 3), (4, 5, 6, 7)]

            def emit(s, k, g):
                for j in range(HG):
                    u = 4 * s + j
                    if k > 0 or j >= 2:
                        act.wait_ge(pT_ready, u - 1)
                    exps(u, j)
                    if k < 15:
                        for p in ORDER[j][0]:
                            if p >= 2:
                                part(s + 1, k + 1, p)
                    if k > 0 or j >= 1:
                        pT(u - 1, (j - 1) % 4)
                    if k < 15:
                        if j == 0:
                            part(s + 1, k + 1, 0)
                        if j == 1:
                            part(s + 1, k + 1, 1)
                        for p in ORDER[j][1]:
                            part(s + 1, k + 1, p)
                    if k > 0 or j >= 2:
                        oT(u - 2, k if j >= 2 else k - 1, (j - 2) % 4)
                    if k % 4 == 2:
                        for i in REPLACED[j]:
                            weight_piece(i, g + 1, (piece_ready, 8 * (s + 1) + i - i % 2 + 2))
                    if k == 5 and j == 0:
                        for i in (8, 9):
                            weight_piece(i, g, (out_ready, s - 1))

            act.wait_ge(x_in, 16)
            for t in range(KT):
                for c in range(2):
                    act.activation(xTh[:, t, c * PIECE:(c + 1) * PIECE], rope_f[:, 2 * t + c, :],
                                   ACT.Copy).then_inc(x_hi, 1)
            for i in range(GP):
                act.wait_ge(raw_in[i % RING], 16 * (i // RING + 1))
                act.activation(weights(i, True), raw[:, i % RING, :], ACT.Copy).then_inc(w_hi, 1)
            for p in range(8):
                part(0, 0, p)
            for s in (0, 1):
                emit(s, s, 0)
            with act.Fori(0, NG - 1) as g:
                for k in range(2, 6):
                    emit(4 * g + k, k, g + k // 4)
            for s in (14, 15):
                emit(s, s, NG - 1)
            last_u = 4 * SLOTS - 1
            pT(last_u, 3)
            oT(last_u - 1, 15, 2)
            oT(last_u, 15, 3)

        @block.vector
        def _(dve):
            def part(s, k, p):
                if p < 2:
                    dve.wait_ge(piece_ready, 8 * s + p + 1)
                    if k > 0 or p:
                        dve.wait_ge(rope_sum, 4 * s + 2 * p)
                    else:
                        dve.wait_ge(x_split, 4)
                        dve.wait_ge(tab_in, 32)
                    bank = PJ[BANK[p]][:, :].rearrange("p (c n) -> p c n", c=2)
                    for f in range(2):
                        table = tables[:, p, f:f + 1, :].broadcast_to([P, 2, S])
                        last = dve.tensor_tensor(rope_f[:, f, :].rearrange("p (c n) -> p c n", c=2), bank, table,
                                                 ALU.mult)
                    last.then_inc(rope_prod, 1)
                else:
                    dve.wait_ge(part_hi, 6 * s + p - 1)
                    dve.tensor_tensor(part_dst(k, p, False), PJ[BANK[p]][:, :],
                                      part_dst(k, p, True).bitcast(F32), ALU.subtract).then_inc(part_split, 1)

            def row_max(u, j):
                dve.wait_ge(scores_ready, u + 1)
                dve.tensor_reduce(rmax[:, j % 2, :], SC[j % 2][:, :, :], axis=AX.X, op=ALU.max).then_inc(rmax_ready, 1)
                dve.wait_ge(rmax_ready, u + 1)
                dve.tensor_scalar(nmax[:, j % 2, :], rmax[:, j % 2, :], -SCALE, None, ALU.mult).then_inc(nmax_ready, 1)

            def normalise(u, j):
                dve.wait_ge(exp_ready, u + 1)
                dve.reciprocal(rinv[:, j % 2, :], rsum[:, j % 2, :]).then_inc(rinv_ready, 1)
                dve.wait_ge(rinv_ready, u + 1)
                for t in range(TT):
                    last = dve.tensor_scalar(probs[:, j % 2, t, :], probs[:, j % 2, t, :], rinv[:, j % 2, t:t + 1],
                                             None, ALU.mult)
                last.then_inc(probs_ready, 1)

            def pT(u, j):
                dve.wait_ge(pT_hi, u + 1)
                dve.tensor_tensor(PTl[:, j % 2, :, :], PT[:, :, :], PTh[:, j % 2, :, :].bitcast(F32),
                                  ALU.subtract).then_inc(pT_split, 1)

            def oT(u, k, j):
                dve.wait_ge(oT_hi, u + 1)
                dve.tensor_tensor(OTl[:, k % 2, j, :], O[:, 0:S], OTh[:, k % 2, j, :].bitcast(F32),
                                  ALU.subtract).then_inc(oT_split, 1)

            def accumulate(s, k):
                dve.wait_ge(out_ready, s + 1)
                if k == 0:
                    dve.wait_ge(res_in, 16)
                else:
                    dve.wait_ge(acc_done, s)
                rows = slice(TT * (k % 4), TT * (k % 4) + TT)
                dve.tensor_tensor(xres[:, rows, :], OUT[:, :, :], xres[:, rows, :], ALU.add).then_inc(acc_done, 1)

            def emit(s, k):
                for j in range(HG):
                    u = 4 * s + j
                    row_max(u, j)
                    if k < 15:
                        for p in ORDER[j][0]:
                            part(s + 1, k + 1, p)
                    normalise(u, j)
                    if k > 0 or j >= 1:
                        pT(u - 1, (j - 1) % 4)
                    if k < 15:
                        for p in ORDER[j][1]:
                            part(s + 1, k + 1, p)
                    if k > 0 or j >= 2:
                        oT(u - 2, k if j >= 2 else k - 1, (j - 2) % 4)
                    if j == 0 and k > 1:
                        accumulate(s - 2, k - 2)

            for t in range(KT):
                for c in range(2):
                    cols = slice(c * PIECE, (c + 1) * PIECE)
                    dve.wait_ge(x_hi, 2 * t + c + 1)
                    dve.tensor_tensor(xTl[:, t, cols], rope_f[:, 2 * t + c, :], xTh[:, t, cols].bitcast(F32),
                                      ALU.subtract).then_inc(x_split, 1)
            for i in range(GP):
                dve.wait_ge(w_hi, i + 1)
                dve.tensor_tensor(weights(i, False), raw[:, i % RING, :], weights(i, True).bitcast(F32),
                                  ALU.subtract).then_inc(w_split, 1)
            for p in range(8):
                part(0, 0, p)
            for s in (0, 1):
                emit(s, s)
            with dve.Fori(0, NG - 1) as g:
                for k in range(2, 6):
                    emit(4 * g + k, k)
            for s in (14, 15):
                emit(s, s)
            last_u = 4 * SLOTS - 1
            accumulate(14, 14)
            pT(last_u, 3)
            oT(last_u - 1, 15, 2)
            oT(last_u, 15, 3)
            accumulate(15, 15)

        @block.gpsimd
        def _(pool):
            def rotate(s, k, p):
                pool.wait_ge(rope_prod, 2 * s + p + 1)
                if k > 0:
                    pool.wait_ge(rope_lo, 2 * s + p - 1)
                c, sn, y = rope_f[:, 0, :], rope_f[:, 1, :], rope_f[:, 2 + p, :]
                pool.tensor_tensor(y[:, 0:S], c[:, 0:S], sn[:, S:2 * S], ALU.subtract).then_inc(rope_sum, 1)
                pool.tensor_tensor(y[:, S:2 * S], c[:, S:2 * S], sn[:, 0:S], ALU.add).then_inc(rope_sum, 1)
                pool.wait_ge(rope_hi, 2 * s + p + 1)
                pool.wait_ge(rope_sum, 4 * s + 2 * p + 2)
                if k > 0:
                    pool.wait_ge(spill_k if p else spill_q, 64 * s)
                pool.tensor_tensor(rot_l[:, p, :, :], y.rearrange("p (c n) -> p c n", c=2),
                                   rot_h[:, p, :, :].bitcast(F32), ALU.subtract).then_inc(rope_lo, 1)

            def split_piece(n, i):
                pool.wait_ge(w_hi, n + 1)
                pool.tensor_tensor(weights(i, False), raw[:, i % RING, :], weights(i, True).bitcast(F32),
                                   ALU.subtract).then_inc(w_split, 1)

            def emit(s, k, g):
                if k < 15:
                    rotate(s + 1, k + 1, 0)
                    rotate(s + 1, k + 1, 1)
                if k % 4 == 2:
                    for i in range(8):
                        split_piece(GP * (g + 1) + i, i)
                if k == 5:
                    for i in (8, 9):
                        split_piece(GP * g + i, i)

            rotate(0, 0, 0)
            rotate(0, 0, 1)
            for s in (0, 1):
                emit(s, s, 0)
            with pool.Fori(0, NG - 1) as g:
                for k in range(2, 6):
                    emit(4 * g + k, k, g + (k // 4))
            for s in (14, 15):
                emit(s, s, 3)
            for i in range(4):
                pool.wait_ge(raw_in[i], 32 * NG + 16 * (FT - RING > i) + 32)
            pool.wait_ge(rope_lo, 2 * SLOTS)
            raw_w = raw[:, 0:4, :].rearrange("p a n -> p (a n)")
            stage_w = rope_f[:, :, :].rearrange("p a n -> p (a n)")
            for i, (src, dst) in enumerate(((raw_w, stage_w), (stage_w, raw_w), (raw_w, stage_w))):
                step = D << i
                a = src.rearrange("p (m two n) -> p m two n", two=2, n=step)
                y = dst.rearrange("p (m two n) -> p m two n", two=2, n=step)
                if i:
                    pool.wait_ge(tiles_done, 2 * i)
                for half, op in ((0, ALU.add), (1, ALU.subtract)):
                    pool.tensor_tensor(y[:, :, half, :], a[:, :, 0, :], a[:, :, 1, :], op).then_inc(tiles_done, 1)


N_LN = {0: 0, 1: 4, 3: 8, 4: 12}
N_RMS = {1: 0, 2: 4}
N_T = {0: 0, 1: 4, 2: 8, 3: 12}
HM, DQ, DH = 8, 16, 32
CAP = 15.0
RMS_EPS = 1e-6
BIG = 1e30
LP = 5
C_N1, C_MH, C_N2, C_SG, C_SU = 0, 2, 4, 6, 14
N_COLS = 22


def layers(nc, keep, had_d, wl_d, wg_d, bg_d, cols_d, mask_d, wm_d, w8_d, sdown_d, out_d):
    xTh, xTl, WBh, WBl, xres, ident, stage = (keep[k] for k in ("xTh", "xTl", "WBh", "WBl", "xres", "ident", "stage"))
    with ExitStack() as ctx:
        def sb(name, shape, dt=F32):
            return ctx.enter_context(nc.sbuf_tensor(name, shape, dt))

        def pb(name, shape=(P, 512)):
            return ctx.enter_context(nc.psum_tensor(name, list(shape), F32))

        def sem(name):
            return ctx.enter_context(nc.semaphore(name))

        WDh, WDl = sb("WDh", [P, FT, D], F32R), sb("WDl", [P, FT, D], F32R)
        WLh, WLl = sb("WLh", [P, LP, PIECE], F32R), sb("WLl", [P, LP, PIECE], F32R)
        WGh, WGl = sb("WGh", [P, KT, 2 * HM], F32R), sb("WGl", [P, KT, 2 * HM], F32R)
        WI = sb("WI", [P, 12, PIECE], F32R)
        fh, fl = sb("fh", [P, FT, S], F32R), sb("fl", [P, FT, S], F32R)
        had = sb("had", [P, P], F32R)
        had_f = sb("had_f", [P, P])
        wg_f = sb("wg_f", [P, KT, 2 * HM])
        raw = sb("raw2", [P, RING, PIECE])
        raw8_words = raw[:, 0:3, :].rearrange("p a n -> p (a n)").bitcast(mybir.dt.int32)
        raw8 = raw8_words.bitcast(I8).rearrange("p (a n) -> p a n", n=PIECE)
        x1 = sb("x1", [P, B * TT, D])
        cols = sb("cols", [P, N_COLS])
        bg = sb("bg", [HM, 2])
        bgs = sb("bgs", [HM, 2])
        mask = sb("mask", [P, P])
        sdown = sb("sdown", [P, D])
        stats = sb("stats", [P, TT, 6])
        mv = sb("mv", [P, TT, 2])
        vare = sb("vare", [P, TT])
        rstd = sb("rstd", [P, TT])
        ssq = sb("ssq", [P, TT])
        mse = sb("mse", [P, TT])
        rrms = sb("rrms", [P, TT])
        mhalf = sb("mhalf", [P, TT * HM])
        xs = sb("xs", [P, TT, D])
        ga, gb = sb("ga", [P, 2, 384]), sb("gb", [P, 2, 384])
        qT, kT = sb("qT", [P, 2, 2, S]), sb("kT", [P, 2, 2, S])
        V1 = sb("V1", [P, 2, TT, HM, DH + 1])
        og = sb("og", [P, 2, TT, D])
        gt = sb("gt", [HM, 2, S])
        cumS, gr, M, nm, ones = (sb(n, [HM, S]) for n in ("cumS", "gr", "M", "nm", "ones"))
        gcol = sb("gcol", [P, TT, HM])
        enm = sb("enm", [P, TT, HM])
        nn, rn, msq, hsc = (sb(n, [P, TT * HM]) for n in ("nn", "rn", "msq", "hsc"))
        ho = sb("ho", [P, TT, D])
        A = stage[:, :].rearrange("p (h n) -> p h n", h=HM)
        scr_m = nc.dram_tensor("scr_m", (B, HM, S), F32).ap()

        UG = [pb(f"UG{i}") for i in range(4)]
        OUTS = pb("OUTS", (P, 2, 512))
        TB = pb("TB")
        X = pb("X")

        names = """had_in wl_in wg_in small_in sdown_in consts_set had_ready w2_hi w2_split had_done wd_hi wd_split
            wg_hi wg_split wl_hi wl_split int8_done wm_hi wm_split
            ln_stats ln_aggr ln_var rstd_ready x_new ssq_ready ms_ready rms_ready xs_ready xs_copied
            xt_ready xt_hi xt_split x_added stored
            qk_ready qk_taken vog_ready v_taken og_ready gates_ready gates_tanh sp_step sp_ready cs_ready gr_ready
            m_ready nm_ready m_out a_in masked rows_ready gcol_ready enm_ready st_ready e_ready c_ready pv_ready
            abs_ready nn_ready rn_ready sq_ready msq_ready hn_step hsc_ready hs_ready ho_ready hoT_ready hoT_hi
            hoT_split wo_ready x1_ready x1_mid int8_in bgs_ready scaled""".split()
        s_ = {n: sem("l_" + n) for n in names}
        wm_in = [sem(f"l_wm_in{i}") for i in range(RING)]
        ffn_sems = [{n: sem(f"f{i}_{n}") for n in ("up", "silu", "gated", "f_hi", "f_lo", "down")} for i in range(3)]

        xh_v = xTh[:, :, :].rearrange("p t (c n) -> p t c n", c=B)
        xl_v = xTl[:, :, :].rearrange("p t (c n) -> p t c n", c=B)
        res_v = xres[:, :, :].rearrange("p (c t) d -> p c t d", c=B)
        x1_v = x1[:, :, :].rearrange("p (c t) d -> p c t d", c=B)

        def settle(eng, *values):
            for v in values:
                if not isinstance(v, int):
                    eng.compute_val(v)
            eng.wait_ge(s_["small_in"], 16 * 4)
            return values

        def dve_stats(dve, k, c):
            l = N_LN[k] + c
            if k:
                added, = settle(dve, l - 3)
                dve.wait_ge(s_["x_added"], added)
            for t in range(TT):
                dve.bn_stats(stats[:, t, :], res_v[:, c, t, :]).then_inc(s_["ln_stats"], 1)
            done, = settle(dve, 2 * l + 2)
            dve.wait_ge(s_["ln_stats"], done)
            for t in range(TT):
                dve.bn_aggr(mv[:, t, :], stats[:, t, :]).then_inc(s_["ln_aggr"], 1)

        def pool_ln(pool, k, c):
            l = N_LN[k] + c
            done, = settle(pool, 2 * l + 2)
            pool.wait_ge(s_["ln_aggr"], done)
            pool.tensor_scalar(vare[:, :], mv[:, :, 1], LN_EPS, None, ALU.add).then_inc(s_["ln_var"], 1)
            pool.wait_ge(s_["ln_var"], l + 1)
            pool.tensor_tensor(rstd[:, :], vare[:, :], mhalf[:, 0:TT], ALU.pow).then_inc(s_["rstd_ready"], 1)

        def dve_apply(dve, k, c):
            l = N_LN[k] + c
            dve.wait_ge(s_["rstd_ready"], l + 1)
            for t in range(TT):
                last = dve.tensor_scalar(res_v[:, c, t, :], res_v[:, c, t, :], mv[:, t, 0:1], rstd[:, t:t + 1],
                                         ALU.subtract, ALU.mult)
            last.then_inc(s_["x_new"], 1)
            if k == 3:
                read, new = settle(dve, N_T[3] + c, l + 1)
                dve.wait_ge(s_["xt_ready"], read)
                dve.wait_ge(s_["x_new"], new)
                dve.tensor_copy(xs[:, :, :], res_v[:, c, :, :]).then_inc(s_["xs_copied"], 1)

        def rms_src(k):
            return res_v if k == 1 else x1_v

        def act_ssq(act, k, c):
            x_done, read = settle(act, (N_LN[1] if k == 1 else 0) + c + 1, N_T[k] + c)
            act.wait_ge(s_["x_new" if k == 1 else "x1_ready"], x_done)
            act.wait_ge(s_["xt_ready"], read)
            for t in range(TT):
                last = act.activation(xs[:, t, :], rms_src(k)[:, c, t, :], ACT.Square, accum_out=ssq[:, t:t + 1])
            last.then_inc(s_["ssq_ready"], 1)

        def pool_rms(pool, k, c):
            m = N_RMS[k] + c
            done, = settle(pool, m + 1)
            pool.wait_ge(s_["ssq_ready"], done)
            pool.tensor_scalar(mse[:, :], ssq[:, :], 1.0 / D, RMS_EPS, ALU.mult, ALU.add).then_inc(s_["ms_ready"], 1)
            pool.wait_ge(s_["ms_ready"], m + 1)
            pool.tensor_tensor(rrms[:, :], mse[:, :], mhalf[:, 0:TT], ALU.pow).then_inc(s_["rms_ready"], 1)

        def dve_xs(dve, k, c):
            m = N_RMS[k] + c
            dve.wait_ge(s_["rms_ready"], m + 1)
            for t in range(TT):
                last = dve.tensor_scalar(xs[:, t, :], rms_src(k)[:, c, t, :], rrms[:, t:t + 1], None, ALU.mult)
            last.then_inc(s_["xs_ready"], 1)

        def pe_T(pe, k, c):
            n = N_T[k] + c
            if k in N_RMS:
                pe.wait_ge(s_["xs_ready"], N_RMS[k] + c + 1)
            elif k == 3:
                pe.wait_ge(s_["xs_copied"], c + 1)
            else:
                pe.wait_ge(s_["x_new"], N_LN[k] + c + 1)
            if not (isinstance(n, int) and n == 0):
                pe.wait_ge(s_["xt_split"], n)
            for f in range(KT):
                for t in range(TT):
                    src = xs[:, t, f * P:(f + 1) * P] if k else res_v[:, c, t, f * P:(f + 1) * P]
                    last = pe.transpose(TB[:, f * S + t * P:f * S + (t + 1) * P], src, ident[:, :])
            last.then_inc(s_["xt_ready"], 1)

        W_COL = {1: C_N1, 2: C_N2}

        def act_hi(act, k, c):
            n = N_T[k] + c
            done, = settle(act, n + 1)
            act.wait_ge(s_["xt_ready"], done)
            tb = TB[:, :].rearrange("p (t n) -> p t n", t=KT)
            if k in W_COL:
                for f in range(KT):
                    last = act.activation(xh_v[:, f, c, :], tb[:, f, :], ACT.Copy,
                                          scale=cols[:, W_COL[k] + f:W_COL[k] + f + 1])
            else:
                last = act.activation(xh_v[:, :, c, :], tb, ACT.Copy)
            last.then_inc(s_["xt_hi"], 1)

        def dve_lo(dve, k, c):
            n = N_T[k] + c
            dve.wait_ge(s_["xt_hi"], n + 1)
            tb = TB[:, :].rearrange("p (t n) -> p t n", t=KT)
            if k in W_COL:
                for f in range(KT):
                    last = dve.scalar_tensor_tensor(xl_v[:, f, c, :], tb[:, f, :], cols[:, W_COL[k] + f:W_COL[k] + f + 1],
                                                    xh_v[:, f, c, :].bitcast(F32), ALU.mult, ALU.subtract)
            else:
                last = dve.tensor_tensor(xl_v[:, :, c, :], tb, xh_v[:, :, c, :].bitcast(F32), ALU.subtract)
            last.then_inc(s_["xt_split"], 1)

        AFTER = {0: 1, 1: 3, 2: 4}
        BEFORE = {0: 0, 1: 2, 2: 3}

        def w_up(kind, t, ht, which, hi=True):
            piece, at = 4 * t + ht // 2, (ht % 2) * 2 * P + which * P
            src = WI if kind == 2 else WBh if hi else WBl
            return src[:, piece, at:at + P]

        def w_down(kind, ht, hi=True):
            if kind == 2:
                return WI[:, FT + ht // 2, (ht % 2) * D:(ht % 2 + 1) * D]
            return (WDh if hi else WDl)[:, ht, :]

        def chunks(eng, kind, step, hook):
            def chunk(c, first):
                for ht in range(FT):
                    step(c, ht, first)
                    if not first:
                        hook(AFTER[kind], c - 1, ht)
                    elif BEFORE[kind]:
                        hook(BEFORE[kind], B - 1, ht)
            chunk(0, True)
            with eng.Fori(1, B) as c:
                chunk(c, False)

        def ffn_pe(pe, kind):
            q = ffn_sems[kind]

            def up(c, ht, first):
                if ht == 0:
                    pe.wait_ge(s_["xt_split"], N_T[BEFORE[kind]] + c + 1)
                if not (first and ht < 4):
                    pe.wait_ge(q["gated"], FT * c + ht - 3)
                elif kind == 0:
                    pe.wait_ge(s_["wd_split"], ht + 1)
                elif kind == 1 and ht == 2:
                    pe.wait_ge(s_["x1_ready"], B)
                for which in range(2):
                    out = UG[ht % 4][:, which * S:(which + 1) * S]
                    for t in range(KT):
                        wh = w_up(kind, t, ht, which)
                        pe.matmul(out, wh, xh_v[:, t, c, :], start=(t == 0), stop=False)
                        last = pe.matmul(out, wh, xl_v[:, t, c, :], start=False, stop=(kind == 2 and t == KT - 1))
                        if kind != 2:
                            last = pe.matmul(out, w_up(kind, t, ht, which, False), xh_v[:, t, c, :],
                                             start=False, stop=(t == KT - 1))
                last.then_inc(q["up"], 1)

            def down(c, ht, first):
                pe.wait_ge(q["f_lo"], FT * c + ht + 1)
                if ht == 0 and not (first and kind == 0):
                    pe.wait_ge(s_["x_added"], N_LN[AFTER[kind]] - 4 + c)
                for t in range(TT):
                    rows = slice(t * P, (t + 1) * P)
                    out = OUTS[:, t, 0:D]
                    pe.matmul(out, fh[:, ht, rows], w_down(kind, ht), start=(ht == 0), stop=False)
                    last = pe.matmul(out, fl[:, ht, rows], w_down(kind, ht), start=False,
                                     stop=(kind == 2 and ht == FT - 1))
                    if kind != 2:
                        last = pe.matmul(out, fh[:, ht, rows], w_down(kind, ht, False), start=False,
                                         stop=(ht == FT - 1))
                last.then_inc(q["down"], 1)

            def step(c, ht, first):
                up(c, ht, first)
                if ht >= 2:
                    down(c, ht - 2, first)
                elif not first:
                    down(c - 1, ht + 6, False)

            def hook(k, c, ht):
                if ht == 5 and k != 4:
                    pe_T(pe, k, c)
            if kind == 1:
                pe.wait_ge(s_["wm_split"], 12)
            if kind == 2:
                pe.wait_ge(s_["int8_done"], 12)
            chunks(pe, kind, step, hook)
            for ht in (6, 7):
                down(B - 1, ht, False)

        def ffn_act(act, kind):
            q = ffn_sems[kind]

            def silu(c, ht, first):
                act.wait_ge(q["up"], FT * c + ht + 1)
                if not (first and ht < 2):
                    act.wait_ge(q["gated"], FT * c + ht - 1)
                scale = cols[:, C_SG + ht:C_SG + ht + 1] if kind == 2 else 1.0
                act.activation(ga[:, ht % 2, 0:S], UG[ht % 4][:, 0:S], ACT.Silu, scale=scale).then_inc(q["silu"], 1)

            def hi(c, ht):
                act.wait_ge(q["gated"], FT * c + ht + 1)
                act.activation(fh[:, ht, :], gb[:, ht % 2, 0:S], ACT.Copy).then_inc(q["f_hi"], 1)

            def step(c, ht, first):
                silu(c, ht, first)
                if ht:
                    hi(c, ht - 1)
                elif not first:
                    hi(c - 1, FT - 1)

            def hook(k, c, ht):
                if ht == 3 and k in N_RMS:
                    act_ssq(act, k, c)
                if ht == 6 and k != 4:
                    act_hi(act, k, c)
            chunks(act, kind, step, hook)
            hi(B - 1, FT - 1)

        def add_out(dve, kind, c):
            q = ffn_sems[kind]
            dve.wait_ge(q["down"], FT * (c + 1))
            src = OUTS[:, :, 0:D]
            if kind == 2:
                dve.wait_ge(s_["x_added"], N_LN[4] - 4 + c)
                dve.wait_ge(s_["xt_ready"], N_T[3] + B)
                dve.tensor_tensor(xs[:, :, :], src, sdown[:, :].rearrange("p (a d) -> p a d", a=1).broadcast_to([P, TT, D]),
                                  ALU.mult).then_inc(s_["scaled"], 1)
                dve.wait_ge(s_["scaled"], c + 1)
                src = xs[:, :, :]
            dve.tensor_tensor(res_v[:, c, :, :], src, res_v[:, c, :, :], ALU.add).then_inc(s_["x_added"], 1)

        def ffn_dve(dve, kind):
            q = ffn_sems[kind]

            def gate(c, ht, first):
                dve.wait_ge(q["silu"], FT * c + ht + 1)
                if not (first and ht < 2):
                    dve.wait_ge(q["f_lo"], FT * c + ht - 1)
                u, y = UG[ht % 4][:, S:2 * S], gb[:, ht % 2, 0:S]
                if kind == 2:
                    dve.scalar_tensor_tensor(y, u, cols[:, C_SU + ht:C_SU + ht + 1], ga[:, ht % 2, 0:S],
                                             ALU.mult, ALU.mult).then_inc(q["gated"], 1)
                else:
                    dve.tensor_tensor(y, u, ga[:, ht % 2, 0:S], ALU.mult).then_inc(q["gated"], 1)

            def lo(c, ht):
                dve.wait_ge(q["f_hi"], FT * c + ht + 1)
                dve.tensor_tensor(fl[:, ht, :], gb[:, ht % 2, 0:S], fh[:, ht, :].bitcast(F32),
                                  ALU.subtract).then_inc(q["f_lo"], 1)

            def step(c, ht, first):
                gate(c, ht, first)
                if ht:
                    lo(c, ht - 1)
                elif not first:
                    lo(c - 1, FT - 1)

            chunks(dve, kind, step, lambda k, c, ht: dve_hook(dve, k, c, ht))
            lo(B - 1, FT - 1)

        KIND_OF = {1: 0, 3: 1, 4: 2}

        def dve_hook(dve, k, c, ht):
            if ht == 1 and k in KIND_OF:
                add_out(dve, KIND_OF[k], c)
            if ht == 2 and k in KIND_OF:
                dve_stats(dve, k, c)
            if ht == 3 and k in KIND_OF:
                dve_apply(dve, k, c)
            if ht == 4 and k in N_RMS:
                dve_xs(dve, k, c)
            if ht == 6 and k != 4:
                dve_lo(dve, k, c)

        def ffn_pool(pool, kind, extra=None):
            def one(k, c):
                if k in KIND_OF:
                    pool_ln(pool, k, c)
                if k in N_RMS:
                    pool_rms(pool, k, c)
            if BEFORE[kind]:
                one(BEFORE[kind], B - 1)
            with pool.Fori(1, B) as c:
                one(AFTER[kind], c - 1)
                if extra:
                    extra(c)

        block = ctx.enter_context(nc.Block())

        @block.sync
        def _(sp):
            sp.dma_start(had_f[:, :], had_d).then_inc(s_["had_in"], 16)
            sp.dma_start(cols[:, :], cols_d).then_inc(s_["small_in"], 16)
            sp.dma_start(bg[:, :], bg_d).then_inc(s_["small_in"], 16)
            sp.dma_start(mask[:, :], mask_d).then_inc(s_["small_in"], 16)
            sp.dma_start(sdown[:, :], sdown_d.broadcast_to([P, D])).then_inc(s_["small_in"], 16)
            sp.dma_start(wg_f[:, :, :], wg_d).then_inc(s_["wg_in"], 16)
            sp.dma_start(raw[:, :, :], wl_d).then_inc(s_["wl_in"], 16)
            sp.wait_ge(s_["wl_split"], LP)
            sp.dma_start(raw8_words, w8_d).then_inc(s_["int8_in"], 16)
            sp.wait_ge(s_["int8_done"], 12)
            for i in range(RING):
                sp.dma_start(raw[:, i, :], wm_d[:, i, :]).then_inc(wm_in[i], 16)

            def m_rows(c):
                sp.wait_ge(s_["m_ready"], c + 1)
                sp.dma_start(scr_m[c], M[:, :]).then_inc(s_["m_out"], 16)
                sp.wait_ge(s_["m_out"], 16 * (c + 1))
                if c:
                    sp.wait_ge(s_["e_ready"], HM * c)
                src = scr_m[c:c + 1]
                sp.dma_start(A[:, :, 0:S], src.broadcast_to([P, HM, S])).then_inc(s_["a_in"], 16)
                sp.dma_start(A[:, :, S:S + P], src[:, :, P:S].broadcast_to([P, HM, P])).then_inc(s_["a_in"], 16)

            def more(lo_, hi_):
                for i in range(lo_, hi_):
                    sp.wait_ge(s_["wm_split"], i - RING + 1)
                    sp.dma_start(raw[:, i % RING, :], wm_d[:, i, :]).then_inc(wm_in[i % RING], 16)
            m_rows(0)
            more(RING, 7)
            m_rows(1)
            more(7, 11)
            m_rows(2)
            more(11, 12)
            m_rows(3)
            with sp.Fori(0, B) as c:
                sp.wait_ge(s_["x_new"], N_LN[4] + c + 1)
                sp.dma_start(out_d.rearrange("(c t p) d -> c p t d", p=P, t=TT)[c], res_v[:, c, :, :]).then_inc(s_["stored"], 16)
            sp.wait_ge(s_["stored"], 16 * B)

        @block.tensor
        def _(pe):
            for c in range(B):
                pe_T(pe, 0, c)
            pe.wait_ge(s_["had_ready"], 1)
            for i in range(4):
                pe.wait_ge(s_["w2_split"], i + 1)
                pe.matmul(UG[i][:, :], had[:, :], WI[:, i, :], start=True, stop=False)
                pe.matmul(UG[i][:, :], had[:, :], WI[:, 4 + i, :], start=False, stop=True).then_inc(s_["had_done"], 1)
            ffn_pe(pe, 0)

            def six(out, lhs, rhs):
                for t in range(KT):
                    pe.matmul(out, lhs[t][0], rhs[t][0], start=(t == 0), stop=False)
                    pe.matmul(out, lhs[t][0], rhs[t][1], start=False, stop=False)
                    last = pe.matmul(out, lhs[t][1], rhs[t][0], start=False, stop=(t == KT - 1))
                return last

            def project(c):
                pe.wait_ge(s_["xt_split"], N_T[1] + c + 1)
                if c == 0:
                    pe.wait_ge(s_["wl_split"], LP)
                    pe.wait_ge(s_["wg_split"], 1)
                x = [(xh_v[:, t, c, :], xl_v[:, t, c, :]) for t in range(KT)]
                for i in range(2):
                    if c == 1:
                        pe.wait_ge(s_["qk_taken"], i + 1)
                    if c >= 2:
                        pe.wait_ge(s_["c_ready"], HM * (c - 1) - 1 + i)
                    for n in range(2):
                        w = slice((2 * i + n) * P, (2 * i + n + 1) * P)
                        last = six(UG[i][:, n * S:(n + 1) * S], [(WLh[:, t, w], WLl[:, t, w]) for t in range(KT)], x)
                    last.then_inc(s_["qk_ready"], 1)
                if c == 1:
                    pe.wait_ge(s_["gates_tanh"], 1)
                if c >= 2:
                    pe.wait_ge(s_["enm_ready"], c - 1)
                for n in range(2):
                    last = six(X[0:HM, n * S:(n + 1) * S],
                               [(WGh[:, t, n * HM:(n + 1) * HM], WGl[:, t, n * HM:(n + 1) * HM]) for t in range(KT)], x)
                last.then_inc(s_["gates_ready"], 1)
                for t in range(TT):
                    if c:
                        pe.wait_ge(s_["og_ready"], 2 * (c - 1) + t + 1)
                    if c == 3:
                        pe.wait_ge(s_["hoT_split"], 1)
                    rows = slice(t * P, (t + 1) * P)
                    six(UG[2 + t][:, :], [(xh_v[:, f, c, rows], xl_v[:, f, c, rows]) for f in range(KT)],
                        [(WLh[:, 2 + f, :], WLl[:, 2 + f, :]) for f in range(KT)]).then_inc(s_["vog_ready"], 1)

            def rows_T(c):
                pe.wait_ge(s_["nm_ready"], c + 1)
                if c < B - 1:
                    pe.wait_ge(s_["gates_tanh"], c + 2)
                else:
                    pe.wait_ge(s_["enm_ready"], c)
                for i, row in enumerate((gr, nm)):
                    for t in range(TT):
                        at = (2 * i + t) * HM
                        last = pe.transpose(X[:, at:at + HM], row[:, t * P:(t + 1) * P], ident[0:HM, 0:HM])
                last.then_inc(s_["rows_ready"], 1)

            def scores(c, h):
                r, i = slice(32 * (h % 4), 32 * (h % 4) + 32), h // 4
                if h == 0:
                    pe.wait_ge(s_["qk_taken"], 2 * min(c + 2, B))
                if h >= 2:
                    pe.wait_ge(s_["c_ready"], HM * c + h - 1)
                bank = UG[h % 2]
                pe.matmul(bank[:, 0:S], kT[r, c % 2, i, 0:P], qT[r, c % 2, i, :], start=True, stop=True)
                pe.matmul(bank[:, S:S + P], kT[r, c % 2, i, P:S], qT[r, c % 2, i, P:S], start=True,
                          stop=True).then_inc(s_["st_ready"], 1)

            def values(c, h):
                pe.wait_ge(s_["c_ready"], HM * c + h + 1)
                if h == 0:
                    pe.wait_ge(s_["v_taken"], 2 * c + 2)
                    if c:
                        pe.wait_ge(s_["hs_ready"], c)
                w, at = gb[:, h % 2, :], slice(h * (DH + 1), (h + 1) * (DH + 1))
                pe.matmul(OUTS[:, 0, at], w[:, 0:P], V1[:, c % 2, 0, h, :], start=True, stop=True)
                pe.matmul(OUTS[:, 1, at], w[:, P:S], V1[:, c % 2, 0, h, :], start=True, stop=False)
                pe.matmul(OUTS[:, 1, at], w[:, S:S + P], V1[:, c % 2, 1, h, :], start=False,
                          stop=True).then_inc(s_["pv_ready"], 1)

            def heads(c):
                scores(c, 0)
                for h in range(HM):
                    if h + 1 < HM:
                        scores(c, h + 1)
                    values(c, h)

            def heads_T(c):
                pe.wait_ge(s_["ho_ready"], c + 1)
                pe.wait_ge(s_["og_ready"], 8 if c else 6)
                for f in range(KT):
                    for t in range(TT):
                        last = pe.transpose(UG[3][:, f * S + t * P:f * S + (t + 1) * P], ho[:, t, f * P:(f + 1) * P],
                                            ident[:, :])
                last.then_inc(s_["hoT_ready"], 1)

            def project_out(c):
                pe.wait_ge(s_["hoT_split"], c + 1)
                pe.wait_ge(s_["og_ready"], 8)
                if c:
                    pe.wait_ge(s_["x1_ready"], c)
                for t in range(TT):
                    rows = slice(t * P, (t + 1) * P)
                    last = six(UG[2][:, t * D:(t + 1) * D], [(fh[:, f, rows], fl[:, f, rows]) for f in range(KT)],
                               [(WLh[:, 4, f * D:(f + 1) * D], WLl[:, 4, f * D:(f + 1) * D]) for f in range(KT)])
                last.then_inc(s_["wo_ready"], 1)

            project(0)
            pe_T(pe, 1, 3)
            project(1)
            rows_T(0)
            heads(0)
            project(2)
            rows_T(1)
            heads(1)
            heads_T(0)
            project(3)
            rows_T(2)
            project_out(0)
            heads(2)
            heads_T(1)
            pe_T(pe, 2, 0)
            project_out(1)
            rows_T(3)
            heads(3)
            heads_T(2)
            pe_T(pe, 2, 1)
            project_out(2)
            heads_T(3)
            pe_T(pe, 2, 2)
            project_out(3)
            ffn_pe(pe, 1)
            ffn_pe(pe, 2)

        @block.scalar
        def _(act):
            act.wait_ge(s_["had_in"], 16)
            act.activation(had[:, :], had_f[:, :], ACT.Copy).then_inc(s_["had_ready"], 1)
            for i in range(4):
                act.activation(WI[:, i, :], stage[:, i * PIECE:(i + 1) * PIECE], ACT.Copy).then_inc(s_["w2_hi"], 1)
            act.wait_ge(s_["wg_in"], 16)
            act.activation(WGh[:, :, :], wg_f[:, :, :], ACT.Copy).then_inc(s_["wg_hi"], 1)
            for c in range(B):
                act_hi(act, 0, c)
            for i in range(4):
                act.wait_ge(s_["had_done"], i + 1)
                act.activation(WDh[:, 2 * i:2 * i + 2, :], UG[i][:, :].rearrange("p (a d) -> p a d", a=2), ACT.Copy,
                               scale=1.0 / 32).then_inc(s_["wd_hi"], 1)
            ffn_act(act, 0)

            def evac(c):
                for i, dst in enumerate((qT, kT)):
                    act.wait_ge(s_["qk_ready"], 2 * c + i + 1)
                    act.activation(dst[:, c % 2, :, :], UG[i][:, :].rearrange("p (i n) -> p i n", i=2),
                                   ACT.Copy).then_inc(s_["qk_taken"], 1)
                act.wait_ge(s_["gates_ready"], c + 1)
                if c == 0:
                    act.wait_ge(s_["bgs_ready"], 1)
                else:
                    act.wait_ge(s_["gr_ready"], c)
                for n in range(2):
                    last = act.activation(gt[:, n, :], X[0:HM, n * S:(n + 1) * S], ACT.Tanh, scale=1.0 / CAP,
                                          bias=bgs[:, n:n + 1])
                last.then_inc(s_["gates_tanh"], 1)
                act.wait_ge(s_["gates_tanh"], c + 1)
                act.activation(gt[:, 1, :], gt[:, 1, :], ACT.Exp, scale=-CAP).then_inc(s_["sp_step"], 1)
                act.wait_ge(s_["sp_step"], c + 1)
                act.activation(gt[:, 1, :], gt[:, 1, :], ACT.Ln, bias=1.0).then_inc(s_["sp_ready"], 1)
                for t in range(TT):
                    act.wait_ge(s_["v_taken"], 2 * c + t + 1)
                    if c >= 2:
                        act.wait_ge(s_["ho_ready"], c - 1)
                    act.activation(og[:, c % 2, t, :], UG[2 + t][:, D:2 * D], ACT.Sigmoid).then_inc(s_["og_ready"], 1)

            def exp_nm(c):
                act.wait_ge(s_["gcol_ready"], c + 1)
                if c:
                    act.wait_ge(s_["nn_ready"], c)
                act.activation(enm[:, :, :], X[:, 2 * HM:4 * HM].rearrange("p (t h) -> p t h", t=TT),
                               ACT.Exp).then_inc(s_["enm_ready"], 1)

            def decays(c):
                for h in range(HM):
                    if h % 4 == 0:
                        act.wait_ge(s_["masked"], 2 * c + h // 4 + 1)
                    if c or h >= 2:
                        act.wait_ge(s_["c_ready"], HM * c + h - 1)
                    e = ga[:, h % 2, :]
                    act.activation(e[:, 0:S], A[:, h, 0:S], ACT.Exp, scale=-1.0, bias=gcol[:, 0, h:h + 1])
                    act.activation(e[:, S:S + P], A[:, h, S:S + P], ACT.Exp, scale=-1.0,
                                   bias=gcol[:, 1, h:h + 1]).then_inc(s_["e_ready"], 1)

            def squares(c):
                act.wait_ge(s_["nn_ready"], c + 1)
                for t in range(TT):
                    last = act.activation(gb[:, t, 0:D].rearrange("p (h n) -> p h n", h=HM),
                                          OUTS[:, t, 0:HM * (DH + 1)].rearrange("p (h n) -> p h n", h=HM)[:, :, 0:DH],
                                          ACT.Square)
                last.then_inc(s_["sq_ready"], 1)

            def hoT(c):
                act.wait_ge(s_["hoT_ready"], c + 1)
                if c:
                    act.wait_ge(s_["wo_ready"], c)
                for f in range(KT):
                    last = act.activation(fh[:, f, :], UG[3][:, f * S:(f + 1) * S], ACT.Copy,
                                          scale=cols[:, C_MH + f:C_MH + f + 1])
                last.then_inc(s_["hoT_hi"], 1)

            act_ssq(act, 1, 3)
            evac(0)
            act_hi(act, 1, 3)
            evac(1)
            exp_nm(0)
            decays(0)
            squares(0)
            evac(2)
            exp_nm(1)
            decays(1)
            squares(1)
            hoT(0)
            evac(3)
            exp_nm(2)
            decays(2)
            squares(2)
            act_ssq(act, 2, 0)
            hoT(1)
            act_hi(act, 2, 0)
            exp_nm(3)
            decays(3)
            squares(3)
            act_ssq(act, 2, 1)
            hoT(2)
            act_hi(act, 2, 1)
            act_ssq(act, 2, 2)
            hoT(3)
            act_hi(act, 2, 2)
            ffn_act(act, 1)
            ffn_act(act, 2)

        @block.vector
        def _(dve):
            dve.memset(ones[:, :], 1.0).then_inc(s_["consts_set"], 1)
            dve.memset(mhalf[:, :], -0.5).then_inc(s_["consts_set"], 1)
            dve.memset(V1[:, :, :, :, DH:DH + 1], 1.0).then_inc(s_["consts_set"], 1)

            def n0(c):
                dve_stats(dve, 0, c)
                dve_apply(dve, 0, c)
            n0(0)
            for i in range(4):
                dve.wait_ge(s_["w2_hi"], i + 1)
                dve.tensor_tensor(WI[:, 4 + i, :], stage[:, i * PIECE:(i + 1) * PIECE], WI[:, i, :].bitcast(F32),
                                  ALU.subtract).then_inc(s_["w2_split"], 1)
            dve_lo(dve, 0, 0)
            for c in range(1, B):
                n0(c)
                dve_lo(dve, 0, c)
            for i in range(4):
                dve.wait_ge(s_["wd_hi"], i + 1)
                pair = WDh[:, 2 * i:2 * i + 2, :]
                dve.scalar_tensor_tensor(WDl[:, 2 * i:2 * i + 2, :], UG[i][:, :].rearrange("p (a d) -> p a d", a=2),
                                         1.0 / 32, pair.bitcast(F32), ALU.mult, ALU.subtract).then_inc(s_["wd_split"], 1)
            dve.wait_ge(s_["wg_hi"], 1)
            dve.tensor_tensor(WGl[:, :, :], wg_f[:, :, :], WGh[:, :, :].bitcast(F32), ALU.subtract).then_inc(s_["wg_split"], 1)
            dve.wait_ge(s_["small_in"], 64)
            dve.tensor_scalar(bgs[:, :], bg[:, :], 1.0 / CAP, None, ALU.mult).then_inc(s_["bgs_ready"], 1)
            ffn_dve(dve, 0)

            def chain(c):
                for t in range(TT):
                    dve.wait_ge(s_["vog_ready"], 2 * c + t + 1)
                    dve.tensor_copy(V1[:, c % 2, t, :, 0:DH], UG[2 + t][:, 0:D].rearrange("p (h n) -> p h n", h=HM))\
                        .then_inc(s_["v_taken"], 1)
                dve.wait_ge(s_["sp_ready"], c + 1)
                if c == 0:
                    dve.wait_ge(s_["consts_set"], 3)
                if c:
                    dve.wait_ge(s_["rows_ready"], c)
                dve.tensor_tensor_scan(cumS[:, :], ones[:, :], gt[:, 1, :], 0.0, ALU.mult, ALU.add).then_inc(s_["cs_ready"], 1)
                dve.wait_ge(s_["cs_ready"], c + 1)
                dve.scalar_tensor_tensor(gr[:, :], gt[:, 0, :], CAP, cumS[:, :], ALU.mult, ALU.add).then_inc(s_["gr_ready"], 1)
                dve.wait_ge(s_["gr_ready"], c + 1)
                if c:
                    dve.wait_ge(s_["m_out"], 16 * c)
                dve.tensor_tensor_scan(M[:, :], ones[:, :], gr[:, :], -BIG, ALU.mult, ALU.max).then_inc(s_["m_ready"], 1)
                dve.wait_ge(s_["m_ready"], c + 1)
                dve.tensor_tensor(nm[:, :], cumS[:, :], M[:, :], ALU.subtract).then_inc(s_["nm_ready"], 1)

            def gates_by_token(c):
                dve.wait_ge(s_["rows_ready"], c + 1)
                if c:
                    dve.wait_ge(s_["e_ready"], HM * c)
                dve.tensor_copy(gcol[:, :, :], X[:, 0:2 * HM].rearrange("p (t h) -> p t h", t=TT)).then_inc(s_["gcol_ready"], 1)

            def weigh(c):
                for h in range(HM):
                    dve.wait_ge(s_["st_ready"], HM * c + h + 1)
                    dve.wait_ge(s_["e_ready"], HM * c + h + 1)
                    if c or h >= 2:
                        dve.wait_ge(s_["pv_ready"], HM * c + h - 1)
                    if c and h == 0:
                        dve.wait_ge(s_["msq_ready"], c)
                    dve.scalar_tensor_tensor(gb[:, h % 2, :], UG[h % 2][:, 0:384], 1.0 / math.sqrt(DQ), ga[:, h % 2, :],
                                             ALU.mult, ALU.mult).then_inc(s_["c_ready"], 1)

            heads_v = OUTS[:, :, 0:HM * (DH + 1)].rearrange("p t (h n) -> p t h n", h=HM)

            def norm_a(c):
                dve.wait_ge(s_["pv_ready"], HM * (c + 1))
                if c:
                    dve.wait_ge(s_["hsc_ready"], c)
                nn_v = nn[:, :].rearrange("p (t h) -> p t h", t=TT)
                dve.wait_ge(s_["enm_ready"], c + 1)
                dve.scalar_tensor_tensor(nn_v, heads_v[:, :, :, DH], -1.0, enm[:, :, :], ALU.mult,
                                         ALU.max).then_inc(s_["abs_ready"], 1)
                dve.wait_ge(s_["abs_ready"], c + 1)
                dve.scalar_tensor_tensor(nn_v, heads_v[:, :, :, DH], 1.0, nn_v, ALU.mult,
                                         ALU.max).then_inc(s_["nn_ready"], 1)
                dve.wait_ge(s_["nn_ready"], c + 1)
                dve.reciprocal(rn[:, :], nn[:, :]).then_inc(s_["rn_ready"], 1)
                dve.wait_ge(s_["sq_ready"], c + 1)
                dve.tensor_reduce(msq[:, :].rearrange("p (t h) -> p t h", t=TT),
                                  gb[:, :, 0:D].rearrange("p t (h n) -> p t h n", h=HM), axis=AX.X,
                                  op=ALU.add).then_inc(s_["msq_ready"], 1)

            def norm_b(c):
                dve.wait_ge(s_["hsc_ready"], c + 1)
                if c:
                    dve.wait_ge(s_["hoT_ready"], c)
                for t in range(TT):
                    sc = hsc[:, t * HM:(t + 1) * HM].rearrange("p (h n) -> p h n", n=1).broadcast_to([P, HM, DH])
                    last = dve.tensor_tensor(ho[:, t, :].rearrange("p (h n) -> p h n", h=HM), heads_v[:, t, :, 0:DH], sc,
                                             ALU.mult)
                last.then_inc(s_["hs_ready"], 1)
                dve.wait_ge(s_["hs_ready"], c + 1)
                dve.wait_ge(s_["og_ready"], 2 * c + 2)
                dve.tensor_tensor(ho[:, :, :], ho[:, :, :], og[:, c % 2, :, :], ALU.mult).then_inc(s_["ho_ready"], 1)

            def hoT(c):
                dve.wait_ge(s_["hoT_hi"], c + 1)
                for f in range(KT):
                    last = dve.scalar_tensor_tensor(fl[:, f, :], UG[3][:, f * S:(f + 1) * S], cols[:, C_MH + f:C_MH + f + 1],
                                                    fh[:, f, :].bitcast(F32), ALU.mult, ALU.subtract)
                last.then_inc(s_["hoT_split"], 1)

            def add_heads(c):
                dve.wait_ge(s_["wo_ready"], c + 1)
                dve.tensor_tensor(x1_v[:, c, :, :], UG[2][:, :].rearrange("p (t d) -> p t d", t=TT), res_v[:, c, :, :],
                                  ALU.add).then_inc(s_["x1_ready"], 1)
                dve.wait_ge(s_["x1_ready"], c + 1)
                dve.tensor_tensor(res_v[:, c, :, :], x1_v[:, c, :, :], res_v[:, c, :, :], ALU.add).then_inc(s_["x1_mid"], 1)

            add_out(dve, 0, 3)
            dve_stats(dve, 1, 3)
            dve_apply(dve, 1, 3)
            dve_xs(dve, 1, 3)
            chain(0)
            dve_lo(dve, 1, 3)
            chain(1)
            gates_by_token(0)
            weigh(0)
            norm_a(0)
            chain(2)
            norm_b(0)
            gates_by_token(1)
            weigh(1)
            norm_a(1)
            hoT(0)
            chain(3)
            norm_b(1)
            add_heads(0)
            gates_by_token(2)
            weigh(2)
            norm_a(2)
            dve_xs(dve, 2, 0)
            hoT(1)
            dve_lo(dve, 2, 0)
            norm_b(2)
            add_heads(1)
            gates_by_token(3)
            weigh(3)
            norm_a(3)
            dve_xs(dve, 2, 1)
            hoT(2)
            dve_lo(dve, 2, 1)
            norm_b(3)
            add_heads(2)
            dve_xs(dve, 2, 2)
            hoT(3)
            dve_lo(dve, 2, 2)
            add_heads(3)
            dve.wait_ge(s_["x1_mid"], 4)
            ffn_dve(dve, 1)
            ffn_dve(dve, 2)
            add_out(dve, 2, 3)
            dve_stats(dve, 4, 3)
            dve_apply(dve, 4, 3)

        @block.gpsimd
        def _(pool):
            pool.wait_ge(s_["consts_set"], 3)
            for c in range(B):
                pool_ln(pool, 0, c)
            pool.wait_ge(s_["wl_in"], 16)
            for i in range(LP):
                pool.tensor_copy(WLh[:, i, :], raw[:, i, :]).then_inc(s_["wl_hi"], 1)
                pool.wait_ge(s_["wl_hi"], i + 1)
                pool.tensor_tensor(WLl[:, i, :], raw[:, i, :], WLh[:, i, :].bitcast(F32), ALU.subtract).then_inc(s_["wl_split"], 1)

            def int8_pieces(c):
                pool.wait_ge(s_["had_done"], 4)
                pool.wait_ge(s_["int8_in"], 16)
                for i in range(4):
                    pool.tensor_copy(WI[:, (c - 1) * 4 + i, :], raw8[:, (c - 1) * 4 + i, :]).then_inc(s_["int8_done"], 1)
            ffn_pool(pool, 0, int8_pieces)
            pool_ln(pool, 1, 3)
            pool_rms(pool, 1, 3)

            def add_mask(c):
                pool.wait_ge(s_["a_in"], 32 * (c + 1))
                for half in range(2):
                    a = A[:, 4 * half:4 * half + 4, :].rearrange("p h (b n) -> p h b n", n=P)[:, :, 0:3:2, :]
                    m = mask[:, :].rearrange("p (a b n) -> p a b n", a=1, b=1).broadcast_to([P, 4, 2, P])
                    pool.tensor_tensor(a, a, m, ALU.add).then_inc(s_["masked"], 1)

            def head_scales(c):
                pool.wait_ge(s_["msq_ready"], c + 1)
                if c:
                    pool.wait_ge(s_["hs_ready"], c)
                base = 4 * c
                pool.tensor_tensor(hsc[:, :], rn[:, :], rn[:, :], ALU.mult).then_inc(s_["hn_step"], 1)
                pool.wait_ge(s_["hn_step"], base + 1)
                pool.tensor_tensor(hsc[:, :], hsc[:, :], msq[:, :], ALU.mult).then_inc(s_["hn_step"], 1)
                pool.wait_ge(s_["hn_step"], base + 2)
                pool.tensor_scalar(hsc[:, :], hsc[:, :], 1.0 / DH, RMS_EPS, ALU.mult, ALU.add).then_inc(s_["hn_step"], 1)
                pool.wait_ge(s_["hn_step"], base + 3)
                pool.tensor_tensor(hsc[:, :], hsc[:, :], mhalf[:, :], ALU.pow).then_inc(s_["hn_step"], 1)
                pool.wait_ge(s_["hn_step"], base + 4)
                pool.tensor_tensor(hsc[:, :], hsc[:, :], rn[:, :], ALU.mult).then_inc(s_["hsc_ready"], 1)

            def split_mlp(lo_, hi_):
                for i in range(lo_, hi_):
                    pool.wait_ge(wm_in[i % RING], 16 * (i // RING + 1))
                    if i == 0:
                        pool.wait_ge(ffn_sems[0]["down"], FT * B)
                    if i < FT:
                        h, l = WBh[:, i, :], WBl[:, i, :]
                    else:
                        at = slice(2 * (i - FT), 2 * (i - FT) + 2)
                        h = WDh[:, at, :].rearrange("p a d -> p (a d)")
                        l = WDl[:, at, :].rearrange("p a d -> p (a d)")
                    pool.tensor_copy(h, raw[:, i % RING, :]).then_inc(s_["wm_hi"], 1)
                    pool.wait_ge(s_["wm_hi"], i + 1)
                    pool.tensor_tensor(l, raw[:, i % RING, :], h.bitcast(F32), ALU.subtract).then_inc(s_["wm_split"], 1)

            add_mask(0)
            split_mlp(0, 2)
            head_scales(0)
            add_mask(1)
            split_mlp(2, 6)
            head_scales(1)
            add_mask(2)
            split_mlp(6, 9)
            head_scales(2)
            pool_rms(pool, 2, 0)
            add_mask(3)
            split_mlp(9, 12)
            head_scales(3)
            pool_rms(pool, 2, 1)
            pool_rms(pool, 2, 2)
            ffn_pool(pool, 1)
            ffn_pool(pool, 2)
            pool_ln(pool, 4, 3)


def _layout(i):
    f = np.float32
    x = i["L0_attn_hidden_states"].reshape(TOK, D)

    def by_kt(m):
        return m.reshape(-1, P, m.shape[1]).transpose(1, 0, 2)

    Wq, Wk, Wv, Wo = (i["L0_attn_" + n] for n in ("Wq", "Wk", "Wv", "Wo"))
    w_att = np.empty((NG, P, GP, PIECE), f)
    for g in range(NG):
        rot = [W[H * DN:].reshape(H, 2, DR // 2, D)[HG * g:HG * g + HG, half].reshape(P, D)
               for W in (Wq, Wk) for half in range(2)]
        w_att[g, :, 0:2] = by_kt(np.concatenate(rot).T)
        for pair in range(2):
            h = HG * g + 2 * pair
            w_att[g, :, 2 + 2 * pair:4 + 2 * pair] = by_kt(
                np.concatenate([W[n * DN:(n + 1) * DN] for n in (h, h + 1) for W in (Wq, Wk)]).T)
        w_att[g, :, 6:8] = by_kt(Wv[g * PIECE:(g + 1) * PIECE].T)
        w_att[g, :, 8:10] = Wo[:, g * PIECE:(g + 1) * PIECE].T.reshape(2, 2, P, D).transpose(2, 0, 1, 3).reshape(P, 2, PIECE)

    def gate_up(gate, up):
        both = np.stack([gate.reshape(D, FT, P), up.reshape(D, FT, P)], 2)
        return both.reshape(KT, P, 4, PIECE).transpose(1, 0, 2, 3).reshape(P, 8, PIECE)

    def down(m):
        return by_kt(m).reshape(P, 4, PIECE)

    def heads(m):
        out = np.zeros((D, HM, 32), f)
        out[:, :, :DQ] = m.reshape(D, HM, DQ)
        return out.reshape(D, 2 * P)

    L1 = {n[8:]: v for n, v in i.items() if n.startswith("L1_attn_")}
    F1 = {n[7:]: v for n, v in i.items() if n.startswith("L1_ffn_")}
    wl = np.empty((P, LP, PIECE), f)
    wl[:, 0:2] = by_kt(np.concatenate([heads(L1["wq"]), heads(L1["wk"])], 1))
    wl[:, 2:4] = by_kt(np.concatenate([L1["wv"], L1["w_og"]], 1))
    wl[:, 4] = by_kt(L1["w_out"]).reshape(P, PIECE)

    t = np.arange(S, dtype=f)[:, None]
    inv = (f(1.0) / f(10000.0) ** (np.arange(0, DR, 2, dtype=f) / f(DR))).astype(f)
    angle = (t * inv).astype(f)
    tab = np.tile(np.stack([np.cos(angle).T, np.sin(angle).T]), (1, HG, 1)).transpose(1, 0, 2)
    rope = np.stack([tab * f(math.sqrt(DN / DR)), tab], 1).astype(f)
    had = np.ones((1, 1), f)
    while len(had) < P:
        had = np.block([[had, had], [had, -had]])
    return {
        "x_tok": x, "x_T": x.T, "w_att": w_att,
        "w_ffn0": gate_up(i["L0_ffn_W1"].T, i["L0_ffn_W3"].T), "w2_raw": down(i["L0_ffn_W2"].T),
        "rope": rope, "ident_d": np.eye(P, dtype=f), "had_d": had,
        "wl_d": wl, "wg_d": by_kt(np.concatenate([L1["w_ig"], L1["w_fg"]], 1)),
        "bg_d": np.stack([L1["b_ig"], L1["b_fg"]], 1),
        "cols_d": np.concatenate([v.reshape(-1, P).T for v in (L1["norm1_w"], L1["mh_w"], L1["norm2_w"], F1["s_gate"], F1["s_up"])], 1),
        "mask_d": np.tril(np.full((P, P), BIG, f), -1),
        "wm_d": np.concatenate([gate_up(L1["w_gate"], L1["w_up"]), down(L1["w_down"])], 1),
        "w8_d": np.ascontiguousarray(
            np.concatenate([gate_up(F1["w_gate"], F1["w_up"]), down(F1["w_down"])], 1).reshape(P, 12 * PIECE)).view(np.int32),
        "sdown_d": F1["s_down"].reshape(1, D),
    }


def build(nc, out_d, x_tok, x_T, w_att, w_ffn0, w2_raw, rope, ident_d, **later):
    with ExitStack() as ctx:
        def sb(name, shape, dt):
            return ctx.enter_context(nc.sbuf_tensor(name, shape, dt))

        keep = {
            "xTh": sb("xTh", [P, KT, TOK], F32R), "xTl": sb("xTl", [P, KT, TOK], F32R),
            "WBh": sb("WBh", [P, FT, PIECE], F32R), "WBl": sb("WBl", [P, FT, PIECE], F32R),
            "xres": sb("xres", [P, B * TT, D], F32), "ident": sb("ident", [P, P], F32),
            "stage": sb("stage", [P, HM * 384], F32),
        }
        attention(nc, keep, x_tok, x_T, w_att, w_ffn0, w2_raw, rope, ident_d)
        layers(nc, keep, out_d=out_d, **later)


def kernel(**inputs):
    import concourse.bacc as bacc
    from concourse.bass_utils import run_bass_kernel_spmd

    nc = bacc.Bacc("TRN2", target_bir_lowering=False, num_devices=1)
    arrays = {n: np.ascontiguousarray(a) for n, a in _layout({n: np.asarray(a) for n, a in inputs.items()}).items()}
    args = {n: nc.dram_tensor("in_" + n, a.shape, mybir.dt.from_np(a.dtype), kind="ExternalInput").ap()
            for n, a in arrays.items()}
    out = nc.dram_tensor("out_x", (TOK, D), F32, kind="ExternalOutput").ap()
    build(nc, out, **args)
    r = run_bass_kernel_spmd(nc, [{"in_" + n: a for n, a in arrays.items()}], core_ids=[0])
    return r.results[0]["out_x"].reshape(B, S, D)
```

```python
import math

import numpy as np
import concourse.bass as bass
from concourse import mybir
from contextlib import ExitStack

F32 = mybir.dt.float32
F32R = mybir.dt.float32r
I8 = mybir.dt.int8
ACT = mybir.ActivationFunctionType
ALU = mybir.AluOpType
AX = mybir.AxisListType

P = 128
B, S, D = 4, 256, 256
TOK = B * S
KT = D // P
TT = S // P
H, DN, DR, DV = 16, 128, 64, 128
HG = 4
NG = H // HG
SLOTS = NG * B
PIECE = 512
GP = 10
RING = 5
FF = 1024
FT = FF // P
SCALE = 1.0 / math.sqrt(DN)
LN_EPS = 1e-5


def attention(nc, keep, x_tok, x_T, w_att, w_ffn0, w2_raw, rope, ident_d, had_d):
    xTh, xTl, WBh, WBl, xres, ident = (keep[k] for k in ("xTh", "xTl", "WBh", "WBl", "xres", "ident"))
    QKh, QKl = keep["QKh"], keep["QKl"]
    rope_f = keep["stage"][:, 0:4 * PIECE].rearrange("p (a n) -> p a n", n=PIECE)
    with ExitStack() as ctx:
        def sb(name, shape, dt):
            return ctx.enter_context(nc.sbuf_tensor(name, shape, dt))

        def pb(name, shape, dt=F32):
            return ctx.enter_context(nc.psum_tensor(name, shape, dt))

        def sem(name):
            return ctx.enter_context(nc.semaphore(name))

        Vh = sb("Vh", [P, 2, TT, PIECE], F32R)
        Vl = sb("Vl", [P, 2, TT, PIECE], F32R)
        Q2 = sb("Q2", [P, 2, HG, S], F32R)
        K2 = sb("K2", [P, 2, HG, S], F32R)
        K3 = sb("K3", [P, 2, HG, S], F32R)
        rot_h = sb("rot_h", [P, 2, 2, S], F32R)
        rot_l = sb("rot_l", [P, 2, 2, S], F32R)
        OTh = sb("OTh", [P, 2, HG, S], F32R)
        OTl = sb("OTl", [P, 2, HG, S], F32R)
        PTh = sb("PTh", [P, 2, TT, S], F32R)
        PTl = sb("PTl", [P, 2, TT, S], F32R)
        raw = sb("raw", [P, RING, PIECE], F32)
        WOh, WOl = sb("WOh", [P, 2, PIECE], F32R), sb("WOl", [P, 2, PIECE], F32R)
        w2t = sb("w2t", [P, FT, D], F32)
        x_raw = w2t[:, :, :].rearrange("p (b t) n -> p b t n", b=B)
        had = keep["stage"][:, 4 * PIECE + D:4 * PIECE + D + P]
        stats = sb("stats0", [P, B - 1, TT, 6], F32)
        mv = sb("mv0", [P, B - 1, TT, 2], F32)
        vare = sb("vare0", [P, B - 1, TT], F32)
        rstd = sb("rstd0", [P, B - 1, TT], F32)
        mhalf = sb("mhalf0", [P, TT], F32)
        tables = sb("tables", [P, 2, 2, S], F32)
        probs = sb("probs", [P, 2, TT, S], F32)
        rmax = sb("rmax", [P, 2, TT], F32)
        nmax = sb("nmax", [P, 2, TT], F32)
        rsum = sb("rsum", [P, 2, TT], F32)
        rinv = sb("rinv", [P, 2, TT], F32)
        scr_q = nc.dram_tensor("scr_q", (2, 4, 32, HG, S), F32).ap()
        scr_k = nc.dram_tensor("scr_k", (2, 4, 32, HG, S), F32).ap()

        SC = [pb(f"SC{i}", [P, TT, S]) for i in range(2)]
        PT = pb("PT", [P, TT, S])
        O = pb("O", [P, 2 * S])
        PJ = [pb(f"PJ{i}", [P, 2 * S]) for i in range(3)]
        OUT = pb("OUT", [P, TT, D])
        BANK = [0, 1, 2, 0, 1, 2, 0, 1]

        x_in = [sem(f"x_in{b}") for b in range(B)]
        tab_in = sem("tab_in")
        res_in = sem("res_in")
        x_hi = sem("x_hi")
        x_split = sem("x_split")
        raw_in = [sem(f"raw_in{i}") for i in range(RING)]
        w_hi = sem("w_hi")
        w_split = sem("w_split")
        piece_ready = sem("piece_ready")
        part_hi = sem("part_hi")
        part_split = sem("part_split")
        rope_prod = sem("rope_prod")
        rope_sum = sem("rope_sum")
        rope_hi = sem("rope_hi")
        rope_lo = sem("rope_lo")
        spill_q = sem("spill_q")
        spill_k = sem("spill_k")
        stack_q = sem("stack_q")
        stack_k = sem("stack_k")
        scores_ready = sem("scores_ready")
        rmax_ready = sem("rmax_ready")
        nmax_ready = sem("nmax_ready")
        exp_ready = sem("exp_ready")
        rinv_ready = sem("rinv_ready")
        probs_ready = sem("probs_ready")
        pT_ready = sem("pT_ready")
        pT_hi = sem("pT_hi")
        pT_split = sem("pT_split")
        head_ready = sem("head_ready")
        oT_hi = sem("oT_hi")
        oT_split = sem("oT_split")
        out_ready = sem("out_ready")
        acc_done = sem("acc_done")
        w2_in = sem("w2_in")
        tiles_done = sem("tiles_done")
        tail_ready = sem("tail_ready")
        tail_hi = sem("tail_hi")
        had_split = sem("had_split")
        xt_split = sem("xt_split")
        mh_set = sem("mh_set")
        ln_stats = sem("ln_stats")
        ln_aggr = sem("ln_aggr")
        ln_var = sem("ln_var")
        rstd_ready = sem("rstd_ready")
        x_new = sem("x_new")


        def weights(i, hi):
            return (WBh if hi else WBl)[:, i, :] if i < 8 else (WOh if hi else WOl)[:, i - 8, :]

        place, spare, butterflies = list(range(FT)), FT, []
        for step in (1, 2, 4):
            for i in range(FT):
                if not i & step:
                    a, b = place[i], place[i + step]
                    butterflies += [(spare, a, b, ALU.add), (b, a, b, ALU.subtract)]
                    place[i], spare = spare, a

        ORDER = [([0, 1], [2]), ([3], [4]), ([5], [6]), ([7], [])]
        EARLY_MAX = (0, 1, 2)
        ACC_STEP = 1
        TAIL = [(0, 1), (2,), (3, 4), (5,)]

        def w2_tile(i):
            return w2t[:, i, :] if i < FT else keep["stage"][:, 4 * PIECE:4 * PIECE + D]

        def w_down(hi, i):
            return (QKh if hi else QKl)[:, 0, i, :]

        def x_chunk(hi, c):
            return (xTh if hi else xTl)[:, :, c * S:(c + 1) * S]

        block = ctx.enter_context(nc.Block())

        @block.sync
        def _(sp):
            def spill(s, k, i):
                scr, spilled = ((scr_q, spill_q), (scr_k, spill_k))[i]
                for part, src, done in ((0, rot_h, rope_hi), (1, rot_l, rope_lo)):
                    sp.wait_ge(done, 2 * s + i + 1)
                    for half in range(2):
                        sp.dma_start(scr[k % 2, 2 * part + half].rearrange("p j n -> j p n"),
                                     src[:, i, half, :].bitcast(F32)).then_inc(spilled, 16)

            def fill(s, k):
                par = k % 2
                sp.wait_ge(piece_ready, 8 * s + 2)
                sp.wait_ge(spill_q, 64 * (s + 1))
                sp.dma_start(Q2[:, par, :, :].bitcast(F32),
                             scr_q[par].rearrange("r p j n -> (r p) j n")).then_inc(stack_q, 16)
                sp.wait_ge(spill_k, 64 * (s + 1))
                for dst, r in ((K2, 0), (K3, 2)):
                    for half in range(2):
                        sp.dma_start(dst[64 * half:64 * half + 64, par, :, :].bitcast(F32),
                                     scr_k[par, r:r + 2].rearrange("r p j n -> (r p) j n")).then_inc(stack_k, 16)

            def load_x(b):
                sp.dma_start(x_raw[:, b, :, :], x_T.rearrange("(t p) (b n) -> b p t n", p=P, b=B)[b]).then_inc(x_in[b], 16)

            def load_first(i):
                sp.dma_start(raw[:, i, :], w_att[0, :, i, :]).then_inc(raw_in[i], 16)
            load_x(0)
            load_first(0)
            load_first(1)
            sp.dma_start(tables[:, :, :, :], rope).then_inc(tab_in, 16)
            for i in range(2, RING):
                load_first(i)
            sp.dma_start(ident[:, :], ident_d).then_inc(tab_in, 16)
            load_x(1)
            for i in range(RING):
                sp.wait_ge(w_split, i + 1)
                sp.dma_start(raw[:, i, :], w_att[0, :, RING + i, :]).then_inc(raw_in[i], 16)
                if i == 1:
                    spill(0, 0, 0)
                if i == 3:
                    spill(0, 0, 1)
            fill(0, 0)
            load_x(2)
            load_x(3)
            sp.dma_start(had, had_d).then_inc(w2_in, 16)
            sp.dma_start(xres[:, :, :], x_tok.rearrange("(t p) d -> p t d", p=P)).then_inc(res_in, 16)

            def emit(s, k):
                group_end = k % 4 == 2
                last_group = k == 14

                def load(i):
                    src = w_ffn0[:, i, :] if last_group else w_att_next(i)
                    sp.dma_start(raw[:, i % RING, :], src).then_inc(raw_in[i % RING], 16)

                def w_att_next(i):
                    return w_att[turn[0] + 1, :, i, :]

                pieces = FT if last_group else GP
                if group_end:
                    for i in range(RING):
                        sp.wait_ge(w_split, GP * (turn[0] + 1) - RING + i + 1)
                        sp.wait_ge(raw_in[i], 32)
                        load(i)
                if k < 15:
                    spill(s + 1, k + 1, 0)
                    spill(s + 1, k + 1, 1)
                    fill(s + 1, k + 1)
                if group_end:
                    for i in range(RING, pieces):
                        sp.wait_ge(w_split, GP * (turn[0] + 1) + i - RING + 1)
                        sp.wait_ge(raw_in[i % RING], 48)
                        load(i)

            sp.wait_ge(x_split, B)
            sp.dma_start(w2t[:, :, :].rearrange("p (a b) d -> p a (b d)", b=2), w2_raw).then_inc(w2_in, 16)
            turn = [0]
            for s in (0, 1):
                emit(s, s)
            with sp.Fori(0, NG - 1) as g:
                turn[0] = g
                for k in range(2, 6):
                    emit(4 * g + k, k)
            turn[0] = NG - 1
            for s in (14, 15):
                emit(s, s)

        @block.tensor
        def _(pe):
            def three(out, lhs, rhs):
                n = len(lhs)
                for i, ((ah, al), (bh, bl)) in enumerate(zip(lhs, rhs)):
                    pe.matmul(out, ah, bh, start=(i == 0), stop=False)
                    pe.matmul(out, ah, bl, start=False, stop=False)
                    last = pe.matmul(out, al, bh, start=False, stop=(i == n - 1))
                return last

            def piece(s, k, p):
                b = k % 4
                out = PJ[BANK[p]]
                toks = slice(b * S, b * S + S)
                if p == 0:
                    pe.wait_ge(x_split, b + 1)
                if k and p < 3:
                    pe.wait_ge(part_split, 6 * s - [1, 0, 2][p])
                if p in (3, 4):
                    pe.wait_ge(rope_prod, 2 * s + p - 2)
                if p > 4:
                    pe.wait_ge(part_split, 6 * s + p - 4)
                if b == 0 and p % 2 == 0:
                    pe.wait_ge(w_split, GP * (s // 4 if isinstance(s, int) else group[0]) + 2 + p)
                if p < 2:
                    for c in range(2):
                        w = slice((2 * p + c) * P, (2 * p + c + 1) * P)
                        last = three(out[:, c * S:(c + 1) * S], [(WBh[:, t, w], WBl[:, t, w]) for t in range(KT)],
                                     [(xTh[:, t, toks], xTl[:, t, toks]) for t in range(KT)])
                elif p < 6:
                    j = p - 2
                    for c in range(2):
                        w = slice((2 * (j % 2) + c) * P, (2 * (j % 2) + c + 1) * P)
                        at = 2 + 2 * (j // 2)
                        last = three(out[:, c * S:(c + 1) * S], [(WBh[:, at + t, w], WBl[:, at + t, w]) for t in range(KT)],
                                     [(xTh[:, t, toks], xTl[:, t, toks]) for t in range(KT)])
                else:
                    rows = slice(b * S + (p - 6) * P, b * S + (p - 5) * P)
                    last = three(out[:, :], [(xTh[:, t, rows], xTl[:, t, rows]) for t in range(KT)],
                                 [(WBh[:, 6 + t, :], WBl[:, 6 + t, :]) for t in range(KT)])
                last.then_inc(piece_ready, 1)

            def scores(s, k, j):
                u, par, bank = 4 * s + j, k % 2, SC[j % 2]
                if j == 0:
                    pe.wait_ge(stack_q, 16 * (s + 1))
                    pe.wait_ge(stack_k, 64 * (s + 1))
                pe.wait_ge(part_split, 6 * s + j + 1)
                if k > 0 or j >= 2:
                    pe.wait_ge(exp_ready, u - 1)
                for t in range(TT):
                    q, keys = slice(t * P, (t + 1) * P), slice(S, 2 * S)
                    out = bank[:, t, :]
                    pe.matmul(out, QKh[:, par, j, q], QKh[:, par, j, keys], start=True, stop=False)
                    pe.matmul(out, QKh[:, par, j, q], QKl[:, par, j, keys], start=False, stop=False)
                    pe.matmul(out, QKl[:, par, j, q], QKh[:, par, j, keys], start=False, stop=False)
                    pe.matmul(out, Q2[:, par, j, q], K2[:, par, j, :], start=False, stop=False)
                    last = pe.matmul(out, Q2[:, par, j, q], K3[:, par, j, :], start=False, stop=True)
                last.then_inc(scores_ready, 1)

            def turn_probs(u, j, first):
                pe.wait_ge(probs_ready, u + 1)
                if not first:
                    pe.wait_ge(pT_split, u)
                for t in range(TT):
                    for c in range(TT):
                        last = pe.transpose(PT[:, c, t * P:(t + 1) * P], probs[:, j % 2, t, c * P:(c + 1) * P],
                                            ident[:, :])
                last.then_inc(pT_ready, 1)

            def values(u, s, k, j, first):
                if j == 0:
                    pe.wait_ge(part_split, 6 * s + 6)
                pe.wait_ge(pT_split, u + 1)
                if not first:
                    pe.wait_ge(oT_split, u)
                heads = slice(j * DV, (j + 1) * DV)
                last = three(O[:, 0:S], [(Vh[:, k % 2, t, heads], Vl[:, k % 2, t, heads]) for t in range(TT)],
                             [(PTh[:, j % 2, t, :], PTl[:, j % 2, t, :]) for t in range(TT)])
                last.then_inc(head_ready, 1)

            def output(s, k, first):
                if k % 4 == 0:
                    pe.wait_ge(w_split, GP * ((s // 4 if isinstance(s, int) else group[0]) + 1))
                pe.wait_ge(oT_split, 4 * s + 4)
                if not first:
                    pe.wait_ge(acc_done, s)
                for t in range(TT):
                    rows = slice(t * P, (t + 1) * P)
                    last = three(OUT[:, t, :], [(OTh[:, k % 2, j, rows], OTl[:, k % 2, j, rows]) for j in range(HG)],
                                 [(WOh[:, j // 2, (j % 2) * D:(j % 2 + 1) * D],
                                   WOl[:, j // 2, (j % 2) * D:(j % 2 + 1) * D]) for j in range(HG)])
                last.then_inc(out_ready, 1)

            def tail(q):
                bank = PJ[q % 3]
                if q < 3:
                    pe.wait_ge(part_split, 6 * SLOTS)
                else:
                    pe.wait_ge(tail_hi, q - 2)
                if q < 4:
                    pe.wait_ge(w2_in, 32)
                    pe.wait_ge(tiles_done, len(butterflies))
                    for i in range(2):
                        last = pe.matmul(bank[:, i * D:(i + 1) * D], had, w2_tile(place[2 * q + i]),
                                         start=True, stop=True)
                else:
                    pe.wait_ge(x_new, q - 3)
                    for f in range(KT):
                        for t in range(TT):
                            last = pe.transpose(bank[:, f * S + t * P:f * S + (t + 1) * P],
                                                xres[:, TT * (q - 4) + t, f * P:(f + 1) * P], ident[:, :])
                last.then_inc(tail_ready, 1)

            def emit(s, k):
                for j in range(HG):
                    u = 4 * s + j
                    scores(s, k, j)
                    if k < 15:
                        for p in ORDER[j][0]:
                            piece(s + 1, k + 1, p)
                    if k > 0 or j >= 1:
                        turn_probs(u - 1, (j - 1) % 4, first=(k == 0 and j == 1))
                    if k < 15:
                        for p in ORDER[j][1]:
                            piece(s + 1, k + 1, p)
                    if j == 3 and k > 0:
                        output(s - 1, k - 1, first=(k == 1))
                    if k > 0 or j >= 2:
                        back = (s, k) if j >= 2 else (s - 1, k - 1)
                        values(u - 2, *back, (j - 2) % 4, first=(k == 0 and j == 2))
                    if k == 15:
                        for q in TAIL[j]:
                            tail(q)

            group = [0]
            for p in range(8):
                piece(0, 0, p)
            for s in (0, 1):
                emit(s, s)
            with pe.Fori(0, NG - 1) as g:
                group[0] = g + 1
                for k in range(2, 6):
                    emit(4 * g + k, k)
            for s in (14, 15):
                emit(s, s)
            last_u = 4 * SLOTS - 1
            turn_probs(last_u, 3, False)
            values(last_u - 1, SLOTS - 1, 15, 2, False)
            values(last_u, SLOTS - 1, 15, 3, False)
            tail(6)
            output(SLOTS - 1, 15, False)


        def part_dst(k, p, hi):
            if p < 6:
                return (QKh if hi else QKl)[:, k % 2, p - 2, :]
            return (Vh if hi else Vl)[:, k % 2, p - 6, :]

        def plan(text):
            return [(word[0], int(word[1:])) for word in text.split()]

        START_ACT = plan("x0 w0 w1 w2 w3 p0 w4 p2 w5 p1 w6 p3 w7 p4 p5 p6 x1 p7 w8 w9 x2 x3")
        START_DVE = plan("x0 w0 w1 p0 w2 w3 p1 w4 p2 w5 w6 p3 w7 p4 p5 p6 x1 p7 w8 w9 x2 x3")

        @block.scalar
        def _(act):
            def part(s, k, p):
                if p < 2:
                    act.wait_ge(rope_sum, 4 * s + 2 * p + 2)
                    if k > 0:
                        act.wait_ge(spill_k if p else spill_q, 64 * s)
                    act.activation(rot_h[:, p, :, :], rope_f[:, 2 + p, :], ACT.Copy).then_inc(rope_hi, 1)
                else:
                    act.wait_ge(piece_ready, 8 * s + p + 1)
                    act.activation(part_dst(k, p, True), PJ[BANK[p]][:, :], ACT.Copy).then_inc(part_hi, 1)

            def exps(u, j):
                act.wait_ge(nmax_ready, u + 1)
                for t in range(TT):
                    last = act.activation(probs[:, j % 2, t, :], SC[j % 2][:, t, :], ACT.Exp, scale=SCALE,
                                          bias=nmax[:, j % 2, t:t + 1], accum_out=rsum[:, j % 2, t:t + 1])
                last.then_inc(exp_ready, 1)

            def pT(u, j):
                act.wait_ge(pT_ready, u + 1)
                act.activation(PTh[:, j % 2, :, :], PT[:, :, :], ACT.Copy).then_inc(pT_hi, 1)

            def oT(u, k, j):
                act.wait_ge(head_ready, u + 1)
                act.activation(OTh[:, k % 2, j, :], O[:, 0:S], ACT.Copy).then_inc(oT_hi, 1)

            def weight_piece(i, g, free):
                act.wait_ge(*free)
                act.wait_ge(raw_in[i % RING], 32 * g + 16 * (i // RING + 1))
                act.activation(weights(i, True), raw[:, i % RING, :], ACT.Copy).then_inc(w_hi, 1)

            def tail(q):
                act.wait_ge(tail_ready, q + 1)
                if q < 4:
                    act.wait_ge(rope_lo, 2 * SLOTS)
                    act.activation(rope_f[:, q, :], PJ[q % 3][:, :], ACT.Copy)
                    act.activation(w_down(True, q), PJ[q % 3][:, :], ACT.Copy).then_inc(tail_hi, 1)
                else:
                    act.activation(x_chunk(True, q - 4), PJ[q % 3][:, :].rearrange("p (t n) -> p t n", t=KT),
                                   ACT.Copy).then_inc(tail_hi, 1)

            REPLACED = [(), (0, 1), (2, 3), (4, 5, 6, 7)]

            def emit(s, k, g):
                for j in range(HG):
                    u = 4 * s + j
                    if k > 0 or j >= 2:
                        act.wait_ge(pT_ready, u - 1)
                    exps(u, j)
                    if k < 15:
                        for p in ORDER[j][0]:
                            if p >= 2:
                                part(s + 1, k + 1, p)
                    if k > 0 or j >= 1:
                        pT(u - 1, (j - 1) % 4)
                    if k < 15:
                        if j == 0:
                            part(s + 1, k + 1, 0)
                        if j == 1:
                            part(s + 1, k + 1, 1)
                        for p in ORDER[j][1]:
                            part(s + 1, k + 1, p)
                    if k > 0 or j >= 2:
                        oT(u - 2, k if j >= 2 else k - 1, (j - 2) % 4)
                    if k == 15:
                        for q in TAIL[j]:
                            tail(q)
                    if k % 4 == 2:
                        for i in REPLACED[j]:
                            weight_piece(i, g + 1, (piece_ready, 8 * (s + 1) + i - i % 2 + 2))
                    if k == 5 and j == 0:
                        for i in (8, 9):
                            weight_piece(i, g, (out_ready, s - 1))

            for what, i in START_ACT:
                if what == "x":
                    act.wait_ge(x_in[i], 16)
                    act.activation(x_chunk(True, i), x_raw[:, i, :, :], ACT.Copy).then_inc(x_hi, 1)
                elif what == "w":
                    act.wait_ge(raw_in[i % RING], 16 * (i // RING + 1))
                    act.activation(weights(i, True), raw[:, i % RING, :], ACT.Copy).then_inc(w_hi, 1)
                else:
                    part(0, 0, i)
            for s in (0, 1):
                emit(s, s, 0)
            with act.Fori(0, NG - 1) as g:
                for k in range(2, 6):
                    emit(4 * g + k, k, g + k // 4)
            for s in (14, 15):
                emit(s, s, NG - 1)
            last_u = 4 * SLOTS - 1
            pT(last_u, 3)
            oT(last_u - 1, 15, 2)
            oT(last_u, 15, 3)
            tail(6)

        @block.vector
        def _(dve):
            def part(s, k, p):
                if p < 2:
                    dve.wait_ge(piece_ready, 8 * s + p + 1)
                    if k > 0 or p:
                        dve.wait_ge(rope_sum, 4 * s + 2 * p)
                    else:
                        dve.wait_ge(tab_in, 32)
                    bank = PJ[BANK[p]][:, :].rearrange("p (c n) -> p c n", c=2)
                    for f in range(2):
                        table = tables[:, p, f:f + 1, :].broadcast_to([P, 2, S])
                        last = dve.tensor_tensor(rope_f[:, f, :].rearrange("p (c n) -> p c n", c=2), bank, table,
                                                 ALU.mult)
                    last.then_inc(rope_prod, 1)
                else:
                    dve.wait_ge(part_hi, 6 * s + p - 1)
                    dve.tensor_tensor(part_dst(k, p, False), PJ[BANK[p]][:, :],
                                      part_dst(k, p, True).bitcast(F32), ALU.subtract).then_inc(part_split, 1)

            def row_max(u, j):
                dve.wait_ge(scores_ready, u + 1)
                dve.tensor_reduce(rmax[:, j % 2, :], SC[j % 2][:, :, :], axis=AX.X, op=ALU.max).then_inc(rmax_ready, 1)
                dve.wait_ge(rmax_ready, u + 1)
                dve.tensor_scalar(nmax[:, j % 2, :], rmax[:, j % 2, :], -SCALE, None, ALU.mult).then_inc(nmax_ready, 1)

            def normalise(u, j):
                dve.wait_ge(exp_ready, u + 1)
                dve.reciprocal(rinv[:, j % 2, :], rsum[:, j % 2, :]).then_inc(rinv_ready, 1)
                dve.wait_ge(rinv_ready, u + 1)
                for t in range(TT):
                    last = dve.tensor_scalar(probs[:, j % 2, t, :], probs[:, j % 2, t, :], rinv[:, j % 2, t:t + 1],
                                             None, ALU.mult)
                last.then_inc(probs_ready, 1)

            def pT(u, j):
                dve.wait_ge(pT_hi, u + 1)
                dve.tensor_tensor(PTl[:, j % 2, :, :], PT[:, :, :], PTh[:, j % 2, :, :].bitcast(F32),
                                  ALU.subtract).then_inc(pT_split, 1)

            def oT(u, k, j):
                dve.wait_ge(oT_hi, u + 1)
                dve.tensor_tensor(OTl[:, k % 2, j, :], O[:, 0:S], OTh[:, k % 2, j, :].bitcast(F32),
                                  ALU.subtract).then_inc(oT_split, 1)

            def accumulate(s, k):
                dve.wait_ge(out_ready, s + 1)
                if k == 0:
                    dve.wait_ge(res_in, 16)
                else:
                    dve.wait_ge(acc_done, s)
                rows = slice(TT * (k % 4), TT * (k % 4) + TT)
                dve.tensor_tensor(xres[:, rows, :], OUT[:, :, :], xres[:, rows, :], ALU.add).then_inc(acc_done, 1)

            def norm_stats(c):
                dve.wait_ge(acc_done, 13 + c)
                for t in range(TT):
                    dve.bn_stats(stats[:, c, t, :], xres[:, TT * c + t, :]).then_inc(ln_stats, 1)
                dve.wait_ge(ln_stats, TT * (c + 1))
                for t in range(TT):
                    dve.bn_aggr(mv[:, c, t, :], stats[:, c, t, :]).then_inc(ln_aggr, 1)

            def norm_apply(c):
                dve.wait_ge(rstd_ready, c + 1)
                for t in range(TT):
                    rows = xres[:, TT * c + t, :]
                    last = dve.tensor_scalar(rows, rows, mv[:, c, t, 0:1], rstd[:, c, t:t + 1],
                                             ALU.subtract, ALU.mult)
                last.then_inc(x_new, 1)

            def split_batch(c):
                dve.wait_ge(tail_hi, 5 + c)
                dve.tensor_tensor(x_chunk(False, c), PJ[(4 + c) % 3][:, :].rearrange("p (t n) -> p t n", t=KT),
                                  x_chunk(True, c).bitcast(F32), ALU.subtract).then_inc(xt_split, 1)

            def emit(s, k):
                for j in range(HG):
                    u = 4 * s + j
                    if not (j and j - 1 in EARLY_MAX):
                        row_max(u, j)
                    if k < 15:
                        for p in ORDER[j][0]:
                            part(s + 1, k + 1, p)
                    if j == ACC_STEP and k > 1:
                        accumulate(s - 2, k - 2)
                    normalise(u, j)
                    if k > 0 or j >= 1:
                        pT(u - 1, (j - 1) % 4)
                    if j in EARLY_MAX:
                        row_max(u + 1, j + 1)
                    if k < 15:
                        for p in ORDER[j][1]:
                            part(s + 1, k + 1, p)
                    if k > 0 or j >= 2:
                        oT(u - 2, k if j >= 2 else k - 1, (j - 2) % 4)
                    if k == 15:
                        if j == 0:
                            norm_stats(0)
                        for q in TAIL[j]:
                            if q >= 4:
                                split_batch(q - 4)
                        if j == 1:
                            norm_apply(0)
                            norm_stats(1)
                        if j == 2:
                            norm_apply(1)

            dve.memset(mhalf[:, :], -0.5).then_inc(mh_set, 1)
            for what, i in START_DVE:
                if what == "x":
                    dve.wait_ge(x_hi, i + 1)
                    dve.tensor_tensor(x_chunk(False, i), x_raw[:, i, :, :], x_chunk(True, i).bitcast(F32),
                                      ALU.subtract).then_inc(x_split, 1)
                elif what == "w":
                    dve.wait_ge(w_hi, i + 1)
                    dve.tensor_tensor(weights(i, False), raw[:, i % RING, :], weights(i, True).bitcast(F32),
                                      ALU.subtract).then_inc(w_split, 1)
                else:
                    part(0, 0, i)
            for s in (0, 1):
                emit(s, s)
            with dve.Fori(0, NG - 1) as g:
                for k in range(2, 6):
                    emit(4 * g + k, k)
            for s in (14, 15):
                emit(s, s)
            last_u = 4 * SLOTS - 1
            pT(last_u, 3)
            accumulate(14, 14)
            norm_stats(2)
            oT(last_u - 1, 15, 2)
            norm_apply(2)
            oT(last_u, 15, 3)
            split_batch(2)
            accumulate(15, 15)

        @block.gpsimd
        def _(pool):
            def rotate(s, k, p):
                pool.wait_ge(rope_prod, 2 * s + p + 1)
                if k > 0:
                    pool.wait_ge(rope_lo, 2 * s + p - 1)
                c, sn, y = rope_f[:, 0, :], rope_f[:, 1, :], rope_f[:, 2 + p, :]
                pool.tensor_tensor(y[:, 0:S], c[:, 0:S], sn[:, S:2 * S], ALU.subtract).then_inc(rope_sum, 1)
                pool.tensor_tensor(y[:, S:2 * S], c[:, S:2 * S], sn[:, 0:S], ALU.add).then_inc(rope_sum, 1)
                pool.wait_ge(rope_hi, 2 * s + p + 1)
                pool.wait_ge(rope_sum, 4 * s + 2 * p + 2)
                if k > 0:
                    pool.wait_ge(spill_k if p else spill_q, 64 * s)
                pool.tensor_tensor(rot_l[:, p, :, :], y.rearrange("p (c n) -> p c n", c=2),
                                   rot_h[:, p, :, :].bitcast(F32), ALU.subtract).then_inc(rope_lo, 1)

            def split_piece(n, i):
                pool.wait_ge(w_hi, n + 1)
                pool.tensor_tensor(weights(i, False), raw[:, i % RING, :], weights(i, True).bitcast(F32),
                                   ALU.subtract).then_inc(w_split, 1)

            def emit(s, k, g):
                if k < 15:
                    rotate(s + 1, k + 1, 0)
                    rotate(s + 1, k + 1, 1)
                if k % 4 == 2:
                    for i in range(8):
                        split_piece(GP * (g + 1) + i, i)
                if k == 5:
                    for i in (8, 9):
                        split_piece(GP * g + i, i)

            rotate(0, 0, 0)
            rotate(0, 0, 1)
            pool.wait_ge(w2_in, 32)
            for s in (0, 1):
                emit(s, s, 0)
                for i in range(12 * s, 12 * s + 12):
                    dst, a, b, op = butterflies[i]
                    if i:
                        pool.wait_ge(tiles_done, i)
                    pool.tensor_tensor(w2_tile(dst), w2_tile(a), w2_tile(b), op).then_inc(tiles_done, 1)
            with pool.Fori(0, NG - 1) as g:
                for k in range(2, 6):
                    emit(4 * g + k, k, g + (k // 4))
            for s in (14, 15):
                emit(s, s, 3)
            pool.wait_ge(mh_set, 1)

            def split_down(q):
                pool.wait_ge(tail_hi, q + 1)
                pool.tensor_tensor(w_down(False, q), rope_f[:, q, :], w_down(True, q).bitcast(F32),
                                   ALU.subtract).then_inc(had_split, 1)

            split_down(0)
            split_down(1)
            for c in range(B - 1):
                pool.wait_ge(ln_aggr, TT * (c + 1))
                pool.tensor_scalar(vare[:, c, :], mv[:, c, :, 1], LN_EPS, None, ALU.add).then_inc(ln_var, 1)
                pool.wait_ge(ln_var, c + 1)
                pool.tensor_tensor(rstd[:, c, :], vare[:, c, :], mhalf[:, :], ALU.pow).then_inc(rstd_ready, 1)
                if c < 2:
                    split_down(2 + c)


N_LN = {0: 1 - B, 1: 1, 3: 1 + B, 4: 1 + 2 * B}
N_RMS = {1: 0, 2: B}
N_T = {0: 1 - B, 1: 1, 2: 1 + B, 3: 1 + 2 * B}
N_ADD = {1: 0, 3: B, 4: 2 * B}
HM, DQ, DH = 8, 16, 32
CAP = 15.0
RMS_EPS = 1e-6
BIG = 1e30
LP = 5
C_N1, C_MH, C_N2, C_SG, C_SU, C_LO, C_SIGN = 0, 2, 4, 6, 14, 22, 23
N_COLS = 24
PAIR = 64 + DH + 1
WIDE = 96 + P


def layers(nc, keep, wl_d, wg_d, bg_d, cols_d, mask_d, wm_d, w8_d, sdown_d, out_d):
    xTh, xTl, WBh, WBl, xres, ident, stage, QKh, QKl = (
        keep[k] for k in ("xTh", "xTl", "WBh", "WBl", "xres", "ident", "stage", "QKh", "QKl"))
    with ExitStack() as ctx:
        def sb(name, shape, dt=F32):
            return ctx.enter_context(nc.sbuf_tensor(name, shape, dt))

        def pb(name, shape=(P, 512)):
            return ctx.enter_context(nc.psum_tensor(name, list(shape), F32))

        def sem(name):
            return ctx.enter_context(nc.semaphore(name))

        def halves(a):
            return [a[:, i, :, :].rearrange("p a (b d) -> p (a b) d", b=2) for i in range(2)]
        (WDh, fh), (WDl, fl) = halves(QKh), halves(QKl)
        WLh, WLl = sb("WLh", [P, LP, PIECE], F32R), sb("WLl", [P, LP, PIECE], F32R)
        WI = sb("WI", [P, 12, PIECE], F32R)
        gate_w = WI[:, :, :].rearrange("p a n -> p (a n)")[:, 12 * PIECE - 4 * KT * WIDE:]
        WGh, WGl = (gate_w[:, i * 2 * KT * WIDE:(i + 1) * 2 * KT * WIDE].rearrange("p (t g n) -> p t g n", t=KT, g=2)
                    for i in range(2))
        raw = sb("raw2", [P, RING, PIECE])
        raw8_words = raw[:, 0:3, :].rearrange("p a n -> p (a n)").bitcast(mybir.dt.int32)
        raw8 = raw8_words.bitcast(I8).rearrange("p (a n) -> p a n", n=PIECE)
        x1 = sb("x1", [P, B * TT, D])
        cols = sb("cols", [P, N_COLS])
        bg = sb("bg", [P, 2])
        bgs = sb("bgs", [P, 2])
        mask = sb("mask", [P, P])
        sdown = sb("sdown", [P, D])
        stats = sb("stats", [P, TT, 6])
        mv = sb("mv", [P, TT, 2])
        vare = sb("vare", [P, TT])
        rstd = sb("rstd", [P, TT])
        ssq = sb("ssq", [P, TT])
        mse = sb("mse", [P, TT])
        rrms = sb("rrms", [P, TT])
        mhalf = sb("mhalf", [P, TT * HM])
        xs = sb("xs", [P, TT, D])
        ga, gb = sb("ga", [P, 2, 384]), sb("gb", [P, 2, 384])
        q_hi = fh[:, 4:6, :].rearrange("p a d -> p (a d)")
        hTh, hTl = fh[:, 6:8, :], fl[:, 6:8, :]
        V1 = sb("V1", [P, B, TT, HM, DH + 1])
        gt = sb("gt", [P, 2, S])
        cumS, gr, M, nm, ones = (sb(n, [P, S]) for n in ("cumS", "gr", "M", "nm", "ones"))
        gcol = sb("gcol", [P, TT, P])
        enm = sb("enm", [P, TT, P])
        nn, n2, msq, hv, hsc = (sb(n, [P, TT * HM]) for n in ("nn", "n2", "msq", "hv", "hsc"))
        hraw = sb("hraw", [P, TT, HM * (DH + 1)])
        ho = sb("ho", [P, TT, D])
        stage1 = sb("stage1", [P, HM * 384])
        wg_f = stage1[:, 0:2 * KT * WIDE].rearrange("p (t g n) -> p t g n", t=KT, g=2)
        A = [a[:, :].rearrange("p (h n) -> p h n", h=HM) for a in (stage, stage1)]
        og_v = x1[:, :, :].rearrange("p (c t) d -> p c t d", c=B)
        scr_m = nc.dram_tensor("scr_m", (B, 32, S), F32).ap()

        UG = [pb(f"UG{i}") for i in range(4)]
        OUTS = pb("OUTS", (P, 2, 512))
        TB = pb("TB")
        X = pb("X")

        names = """wl_in wg_in small_in consts_set wg_hi wg_split wl_hi wl_split int8_in int8_done wm_hi wm_split
            ln_stats ln_aggr ln_var rstd_ready x_new ssq_ready ms_ready rms_ready xs_ready xs_copied
            xt_ready xt_hi xt_split x_added scaled stored
            bgs_ready qk_ready qk_hi qk_split vog_ready v_taken og_ready gates_ready gates_tanh sp_step sp_ready
            cs_ready gr_ready m_ready nm_ready m_out masked rows_ready gcol_ready enm_ready
            st_ready e_ready c_ready pv_ready vt_ready back_ready taken abs_ready nn_ready n2_ready sq_ready sum_ready msq_ready
            hsc_ready hs_ready ho_ready hoT_ready hoT_hi hoT_split wo_ready x1_ready x1_mid""".split()
        s_ = {n: sem("l_" + n) for n in names}
        a_in = [sem(f"l_a_in{i}") for i in range(2)]
        wm_in = [sem(f"l_wm_in{i}") for i in range(RING)]
        ffn_sems = [{n: sem(f"f{i}_{n}") for n in ("up", "silu", "gated", "f_hi", "f_lo", "down")} for i in range(3)]

        xh_v = xTh[:, :, :].rearrange("p t (c n) -> p t c n", c=B)
        xl_v = xTl[:, :, :].rearrange("p t (c n) -> p t c n", c=B)
        res_v = xres[:, :, :].rearrange("p (c t) d -> p c t d", c=B)
        x1_v = x1[:, :, :].rearrange("p (c t) d -> p c t d", c=B)

        def settle(eng, *values):
            for v in values:
                if not isinstance(v, int):
                    eng.compute_val(v)
            eng.wait_ge(s_["small_in"], 16 * 4)
            return values

        def dve_stats(dve, k, c):
            l = N_LN[k] + c
            if k:
                added, = settle(dve, N_ADD[k] + c + 1)
                dve.wait_ge(s_["x_added"], added)
            for t in range(TT):
                dve.bn_stats(stats[:, t, :], res_v[:, c, t, :]).then_inc(s_["ln_stats"], 1)
            done, = settle(dve, 2 * l + 2)
            dve.wait_ge(s_["ln_stats"], done)
            for t in range(TT):
                dve.bn_aggr(mv[:, t, :], stats[:, t, :]).then_inc(s_["ln_aggr"], 1)

        def pool_ln(pool, k, c):
            l = N_LN[k] + c
            done, = settle(pool, 2 * l + 2)
            pool.wait_ge(s_["ln_aggr"], done)
            pool.tensor_scalar(vare[:, :], mv[:, :, 1], LN_EPS, None, ALU.add).then_inc(s_["ln_var"], 1)
            pool.wait_ge(s_["ln_var"], l + 1)
            pool.tensor_tensor(rstd[:, :], vare[:, :], mhalf[:, 0:TT], ALU.pow).then_inc(s_["rstd_ready"], 1)

        def dve_apply(dve, k, c):
            l = N_LN[k] + c
            dve.wait_ge(s_["rstd_ready"], l + 1)
            for t in range(TT):
                last = dve.tensor_scalar(res_v[:, c, t, :], res_v[:, c, t, :], mv[:, t, 0:1], rstd[:, t:t + 1],
                                         ALU.subtract, ALU.mult)
            last.then_inc(s_["x_new"], 1)
            if k == 3:
                read, new = settle(dve, N_T[3] + c, l + 1)
                dve.wait_ge(s_["xt_ready"], read)
                dve.wait_ge(s_["x_new"], new)
                dve.tensor_copy(xs[:, :, :], res_v[:, c, :, :]).then_inc(s_["xs_copied"], 1)

        def rms_src(k):
            return res_v if k == 1 else x1_v

        def act_ssq(act, k, c):
            x_done, read = settle(act, (N_LN[1] if k == 1 else 0) + c + 1, N_T[k] + c)
            act.wait_ge(s_["x_new" if k == 1 else "x1_ready"], x_done)
            act.wait_ge(s_["xt_ready"], read)
            for t in range(TT):
                last = act.activation(xs[:, t, :], rms_src(k)[:, c, t, :], ACT.Square, accum_out=ssq[:, t:t + 1])
            last.then_inc(s_["ssq_ready"], 1)

        def pool_rms(pool, k, c):
            m = N_RMS[k] + c
            done, = settle(pool, m + 1)
            pool.wait_ge(s_["ssq_ready"], done)
            pool.tensor_scalar(mse[:, :], ssq[:, :], 1.0 / D, RMS_EPS, ALU.mult, ALU.add).then_inc(s_["ms_ready"], 1)
            pool.wait_ge(s_["ms_ready"], m + 1)
            pool.tensor_tensor(rrms[:, :], mse[:, :], mhalf[:, 0:TT], ALU.pow).then_inc(s_["rms_ready"], 1)

        def dve_xs(dve, k, c):
            m = N_RMS[k] + c
            dve.wait_ge(s_["rms_ready"], m + 1)
            for t in range(TT):
                last = dve.tensor_scalar(xs[:, t, :], rms_src(k)[:, c, t, :], rrms[:, t:t + 1], None, ALU.mult)
            last.then_inc(s_["xs_ready"], 1)

        def pe_T(pe, k, c):
            n = N_T[k] + c
            if k in N_RMS:
                pe.wait_ge(s_["xs_ready"], N_RMS[k] + c + 1)
            elif k == 3:
                pe.wait_ge(s_["xs_copied"], c + 1)
            else:
                pe.wait_ge(s_["x_new"], N_LN[k] + c + 1)
            if not (isinstance(n, int) and n == 0):
                pe.wait_ge(s_["xt_split"], n)
            for f in range(KT):
                for t in range(TT):
                    src = xs[:, t, f * P:(f + 1) * P] if k else res_v[:, c, t, f * P:(f + 1) * P]
                    last = pe.transpose(TB[:, f * S + t * P:f * S + (t + 1) * P], src, ident[:, :])
            last.then_inc(s_["xt_ready"], 1)

        W_COL = {1: C_N1, 2: C_N2}

        def act_hi(act, k, c):
            n = N_T[k] + c
            done, = settle(act, n + 1)
            act.wait_ge(s_["xt_ready"], done)
            tb = TB[:, :].rearrange("p (t n) -> p t n", t=KT)
            if k in W_COL:
                for f in range(KT):
                    last = act.activation(xh_v[:, f, c, :], tb[:, f, :], ACT.Copy,
                                          scale=cols[:, W_COL[k] + f:W_COL[k] + f + 1])
            else:
                last = act.activation(xh_v[:, :, c, :], tb, ACT.Copy)
            last.then_inc(s_["xt_hi"], 1)

        def dve_lo(dve, k, c):
            n = N_T[k] + c
            dve.wait_ge(s_["xt_hi"], n + 1)
            tb = TB[:, :].rearrange("p (t n) -> p t n", t=KT)
            if k in W_COL:
                for f in range(KT):
                    last = dve.scalar_tensor_tensor(xl_v[:, f, c, :], tb[:, f, :], cols[:, W_COL[k] + f:W_COL[k] + f + 1],
                                                    xh_v[:, f, c, :].bitcast(F32), ALU.mult, ALU.subtract)
            else:
                last = dve.tensor_tensor(xl_v[:, :, c, :], tb, xh_v[:, :, c, :].bitcast(F32), ALU.subtract)
            last.then_inc(s_["xt_split"], 1)

        LAG = 3
        T_STEP = {0: 5, 1: 6, 3: 5, 4: FT}
        AFTER = {0: 1, 1: 3, 2: 4}
        BEFORE = {0: 0, 1: 2, 2: 3}

        def w_up(kind, t, ht, which, hi=True):
            piece, at = 4 * t + ht // 2, (ht % 2) * 2 * P + which * P
            src = WI if kind == 2 else WBh if hi else WBl
            return src[:, piece, at:at + P]

        def w_down(kind, ht, hi=True):
            if kind == 2:
                return WI[:, FT + ht // 2, (ht % 2) * D:(ht % 2 + 1) * D]
            return (WDh if hi else WDl)[:, ht, :]

        def chunks(eng, kind, step, hook, first_hook=None):
            def chunk(c, first):
                for ht in range(FT):
                    step(c, ht, first)
                    if not first:
                        hook(AFTER[kind], c - 1, ht)
                    else:
                        (first_hook or hook)(BEFORE[kind], B - 1, ht)
            chunk(0, True)
            with eng.Fori(1, B) as c:
                chunk(c, False)

        def ffn_pe(pe, kind, first_hook=None):
            q = ffn_sems[kind]

            def up(c, ht, first):
                if ht == 0 and not (first and kind == 0):
                    pe.wait_ge(s_["xt_split"], 1 if kind == 0 else N_T[BEFORE[kind]] + c + 1)
                if not (first and ht < 4):
                    pe.wait_ge(q["gated"], FT * c + ht - 3)
                for which in range(2):
                    out = UG[ht % 4][:, which * S:(which + 1) * S]
                    for t in range(KT):
                        wh = w_up(kind, t, ht, which)
                        pe.matmul(out, wh, xh_v[:, t, c, :], start=(t == 0), stop=False)
                        last = pe.matmul(out, wh, xl_v[:, t, c, :], start=False, stop=(kind == 2 and t == KT - 1))
                        if kind != 2:
                            last = pe.matmul(out, w_up(kind, t, ht, which, False), xh_v[:, t, c, :],
                                             start=False, stop=(t == KT - 1))
                last.then_inc(q["up"], 1)

            def down(c, ht, first):
                if ht == 1:
                    down(c, 0, first)
                pe.wait_ge(q["f_lo"], FT * c + ht + 1)
                if ht == 0 and not (first and kind == 0):
                    if kind == 2 and not first:
                        pe.wait_ge(s_["scaled"], c)
                    elif kind == 1 and first:
                        pe.wait_ge(s_["taken"], B)
                    else:
                        pe.wait_ge(s_["x_added"], N_ADD[AFTER[kind]] + c)
                for t in range(TT):
                    rows = slice(t * P, (t + 1) * P)
                    out = OUTS[:, t, 0:D]
                    pe.matmul(out, fh[:, ht, rows], w_down(kind, ht), start=(ht == 0), stop=False)
                    last = pe.matmul(out, fl[:, ht, rows], w_down(kind, ht), start=False,
                                     stop=(kind == 2 and ht == FT - 1))
                    if kind != 2:
                        last = pe.matmul(out, fh[:, ht, rows], w_down(kind, ht, False), start=False,
                                         stop=(ht == FT - 1))
                last.then_inc(q["down"], 1)

            def step(c, ht, first):
                up(c, ht, first)
                if ht > LAG:
                    down(c, ht - LAG, first)
                elif ht < LAG and not first:
                    down(c - 1, ht + FT - LAG, False)

            def hook(k, c, ht):
                if ht == T_STEP[k]:
                    pe_T(pe, k, c)
            if kind == 1:
                pe.wait_ge(s_["wm_split"], 12)
            if kind == 2:
                pe.wait_ge(s_["int8_done"], 12)
            chunks(pe, kind, step, hook, first_hook)
            for ht in range(FT - LAG, FT):
                down(B - 1, ht, False)

        def ffn_act(act, kind, first_hook=None):
            q = ffn_sems[kind]

            def silu(c, ht, first):
                act.wait_ge(q["up"], FT * c + ht + 1)
                if not (first and ht < 2):
                    act.wait_ge(q["gated"], FT * c + ht - 1)
                scale = cols[:, C_SG + ht:C_SG + ht + 1] if kind == 2 else 1.0
                act.activation(ga[:, ht % 2, 0:S], UG[ht % 4][:, 0:S], ACT.Silu, scale=scale).then_inc(q["silu"], 1)

            def hi(c, ht):
                act.wait_ge(q["gated"], FT * c + ht + 1)
                act.activation(fh[:, ht, :], gb[:, ht % 2, 0:S], ACT.Copy).then_inc(q["f_hi"], 1)

            def step(c, ht, first):
                silu(c, ht, first)
                if ht:
                    hi(c, ht - 1)
                elif not first:
                    hi(c - 1, FT - 1)

            def hook(k, c, ht):
                if ht == 3 and k in N_RMS:
                    act_ssq(act, k, c)
                if ht == T_STEP[k] + 1:
                    act_hi(act, k, c)
            chunks(act, kind, step, hook, first_hook)
            hi(B - 1, FT - 1)

        def add_out(dve, kind, c):
            q = ffn_sems[kind]
            dve.wait_ge(q["down"], FT * (c + 1))
            src = OUTS[:, :, 0:D]
            if kind == 1:
                dve.wait_ge(s_["x1_mid"], B)
            if kind == 2:
                dve.wait_ge(s_["x_added"], N_ADD[4] + c)
                dve.wait_ge(s_["xt_ready"], N_T[3] + B)
                dve.tensor_tensor(xs[:, :, :], src, sdown[:, :].rearrange("p (a d) -> p a d", a=1).broadcast_to([P, TT, D]),
                                  ALU.mult).then_inc(s_["scaled"], 1)
                dve.wait_ge(s_["scaled"], c + 1)
                src = xs[:, :, :]
            dve.tensor_tensor(res_v[:, c, :, :], src, res_v[:, c, :, :], ALU.add).then_inc(s_["x_added"], 1)

        def ffn_dve(dve, kind, first_hook=None):
            q = ffn_sems[kind]

            def gate(c, ht, first):
                dve.wait_ge(q["silu"], FT * c + ht + 1)
                if not (first and ht < 2):
                    dve.wait_ge(q["f_lo"], FT * c + ht - 1)
                u, y = UG[ht % 4][:, S:2 * S], gb[:, ht % 2, 0:S]
                if kind == 2:
                    dve.scalar_tensor_tensor(y, u, cols[:, C_SU + ht:C_SU + ht + 1], ga[:, ht % 2, 0:S],
                                             ALU.mult, ALU.mult).then_inc(q["gated"], 1)
                else:
                    dve.tensor_tensor(y, u, ga[:, ht % 2, 0:S], ALU.mult).then_inc(q["gated"], 1)

            def lo(c, ht):
                dve.wait_ge(q["f_hi"], FT * c + ht + 1)
                dve.tensor_tensor(fl[:, ht, :], gb[:, ht % 2, 0:S], fh[:, ht, :].bitcast(F32),
                                  ALU.subtract).then_inc(q["f_lo"], 1)

            def step(c, ht, first):
                gate(c, ht, first)
                if ht:
                    lo(c, ht - 1)
                elif not first:
                    lo(c - 1, FT - 1)

            chunks(dve, kind, step, lambda k, c, ht: dve_hook(dve, k, c, ht), first_hook)
            lo(B - 1, FT - 1)

        AT = dict(take=0, squares=2, norm_a=2, norm_b=4, heads_T=5, hoT_hi=7, hoT_lo=7, out=7,
                  ssq=3, xs=3, T=4, hi=5)
        MLP_PIECES = (3, 2, 2)

        def stack(c, i):
            return WI[:, 3 * c + i, :]

        heads_v = OUTS[:, :, :].rearrange("p t (h n) -> p t h n", h=HM)[:, :, :, 0:DH + 1]
        gate_sums = (X[:, 0:S], OUTS[:, 1, 0:S])
        hraw_v = hraw[:, :, :].rearrange("p t (h n) -> p t h n", h=HM)

        def mlp_place(i, hi):
            if i < FT:
                return (WBh if hi else WBl)[:, i, :]
            at = slice(2 * (i - FT), 2 * (i - FT) + 2)
            return (WDh if hi else WDl)[:, at, :].rearrange("p a d -> p (a d)")

        KIND_OF = {1: 0, 3: 1, 4: 2}

        def dve_hook(dve, k, c, ht):
            if ht == 2 and k in KIND_OF:
                add_out(dve, KIND_OF[k], c)
            if ht == (4 if k == 4 else 2) and k != 2:
                dve_stats(dve, k, c)
            if ht == (6 if k == 4 else 3) and k != 2:
                dve_apply(dve, k, c)
            if ht == 4 and k in N_RMS:
                dve_xs(dve, k, c)
            if ht == T_STEP[k] + 1 and k != 4:
                dve_lo(dve, k, c)

        def ffn_pool(pool, kind, extra=None):
            def one(k, c):
                if k != 2:
                    pool_ln(pool, k, c)
                if k in N_RMS:
                    pool_rms(pool, k, c)
            if kind:
                one(BEFORE[kind], B - 1)
            with pool.Fori(1, B) as c:
                one(AFTER[kind], c - 1)
                if extra:
                    extra(c)

        block = ctx.enter_context(nc.Block())

        @block.sync
        def _(sp):
            sp.dma_start(cols[:, :], cols_d).then_inc(s_["small_in"], 16)
            sp.dma_start(bg[:, :], bg_d).then_inc(s_["small_in"], 16)
            sp.dma_start(mask[:, :], mask_d).then_inc(s_["small_in"], 16)
            sp.dma_start(sdown[:, :], sdown_d.broadcast_to([P, D])).then_inc(s_["small_in"], 16)
            sp.dma_start(stage1[:, 0:2 * KT * WIDE], wg_d).then_inc(s_["wg_in"], 16)
            sp.dma_start(raw[:, :, :], wl_d).then_inc(s_["wl_in"], 16)
            for i in range(RING):
                sp.wait_ge(s_["wl_split"], i + 1)
                sp.dma_start(raw[:, i, :], wm_d[:, i, :]).then_inc(wm_in[i], 16)

            def m_rows(c):
                if c > 1:
                    sp.wait_ge(s_["e_ready"], HM * (c - 1))
                src = scr_m[c:c + 1, 0:HM, :]
                sp.dma_start(A[c % 2][:, :, 0:S], src.broadcast_to([P, HM, S])).then_inc(a_in[c % 2], 16)
                sp.dma_start(A[c % 2][:, :, S:S + P], src[:, :, P:S].broadcast_to([P, HM, P])).then_inc(a_in[c % 2], 16)

            def more(lo_, hi_):
                for i in range(lo_, hi_):
                    sp.wait_ge(s_["wm_split"], i - RING + 1)
                    sp.wait_ge(wm_in[i % RING], 16 * (i // RING))
                    sp.dma_start(raw[:, i % RING, :], wm_d[:, i, :]).then_inc(wm_in[i % RING], 16)
            sp.wait_ge(s_["m_ready"], 1)
            sp.dma_start(scr_m.rearrange("c h n -> (c h) n"), M[:, :]).then_inc(s_["m_out"], 16)
            sp.wait_ge(s_["m_out"], 16)
            m_rows(0)
            m_rows(1)
            more(RING, 10)
            m_rows(2)
            more(10, 12)
            m_rows(3)
            sp.wait_ge(s_["wm_split"], 12)
            sp.dma_start(raw8_words, w8_d).then_inc(s_["int8_in"], 16)
            with sp.Fori(0, B) as c:
                sp.wait_ge(s_["x_new"], N_LN[4] + c + 1)
                sp.dma_start(out_d.rearrange("(c t p) d -> c p t d", p=P, t=TT)[c], res_v[:, c, :, :]).then_inc(s_["stored"], 16)
            sp.wait_ge(s_["stored"], 16 * B)

        @block.tensor
        def _(pe):
            ffn_pe(pe, 0)

            def six(out, lhs, rhs):
                for t in range(KT):
                    pe.matmul(out, lhs[t][0], rhs[t][0], start=(t == 0), stop=False)
                    pe.matmul(out, lhs[t][0], rhs[t][1], start=False, stop=False)
                    last = pe.matmul(out, lhs[t][1], rhs[t][0], start=False, stop=(t == KT - 1))
                return last

            def x_parts(c):
                return [(xh_v[:, t, c, :], xl_v[:, t, c, :]) for t in range(KT)]

            def project_gates(c):
                pe.wait_ge(s_["xt_split"], N_T[1] + c + 1)
                if c == 0:
                    pe.wait_ge(s_["wg_split"], 1)
                    pe.wait_ge(s_["x_added"], N_ADD[3])
                w = slice(96 - 32 * c, 96 - 32 * c + P)
                for n, out in enumerate(gate_sums):
                    for i in range(3 * KT):
                        t, (a, b) = i // 3, ((WGh, xh_v), (WGh, xl_v), (WGl, xh_v))[i % 3]
                        last = pe.matmul(out, a[:, t, n, w], b[:, t, c, :], start=(c == 0 and i == 0),
                                         stop=(c == B - 1 and i == 3 * KT - 1))
                last.then_inc(s_["gates_ready"], 1)

            def project(c):
                if c == 0:
                    pe.wait_ge(s_["wl_split"], LP - 1)
                for i in range(2):
                    if c:
                        pe.wait_ge(s_["qk_split"], 2 * c - 1 + i)
                    for n in range(2):
                        w = slice((2 * i + n) * P, (2 * i + n + 1) * P)
                        last = six(UG[i][:, n * S:(n + 1) * S], [(WLh[:, t, w], WLl[:, t, w]) for t in range(KT)],
                                   x_parts(c))
                    last.then_inc(s_["qk_ready"], 1)
                for t in range(TT):
                    if c:
                        pe.wait_ge(s_["og_ready"], 2 * (c - 1) + t + 1)
                    rows = slice(t * P, (t + 1) * P)
                    six(UG[2 + t][:, :], [(xh_v[:, f, c, rows], xl_v[:, f, c, rows]) for f in range(KT)],
                        [(WLh[:, 2 + f, :], WLl[:, 2 + f, :]) for f in range(KT)]).then_inc(s_["vog_ready"], 1)

            def rows_T():
                pe.wait_ge(s_["nm_ready"], 1)
                for i, row in enumerate((gr, nm)):
                    for t in range(TT):
                        at = (2 * i + t) * P
                        last = pe.transpose(X[:, at:at + P], row[:, t * P:(t + 1) * P], ident[:, :])
                last.then_inc(s_["rows_ready"], 1)

            def scores(c, h):
                r, n = slice(32 * (h % 4), 32 * (h % 4) + 32), (h // 4) * S
                if h == 0:
                    pe.wait_ge(s_["qk_split"], 2 * B if c == 0 else 2 * (c + 1))
                if c or h >= 2:
                    pe.wait_ge(s_["c_ready"], HM * c + h - 1)
                bank = UG[h % 2]
                for keys, q, out in ((n, slice(n, n + S), bank[:, 0:S]), (n + P, slice(n + P, n + S), bank[:, S:S + P])):
                    pe.matmul(out, stack(c, 1)[r, keys:keys + P], stack(c, 0)[r, q], start=True, stop=False)
                    last = pe.matmul(out, stack(c, 2)[r, keys:keys + P], stack(c, 0)[r, q], start=False, stop=True)
                last.then_inc(s_["st_ready"], 1)

            def values(c, h):
                pe.wait_ge(s_["c_ready"], HM * c + h + 1)
                if c or h >= 4:
                    pe.wait_ge(s_["vt_ready"], HM // 2 * c + h // 2 - 1)
                w = gb[:, h % 2, :]
                out = UG[2 + h // 2 % 2][0:DH + 1, h % 2 * S:(h % 2 + 1) * S]
                pe.matmul(out[:, 0:P], V1[:, c, 0, h, :], w[:, 0:P], start=True, stop=True)
                pe.matmul(out[:, P:S], V1[:, c, 0, h, :], w[:, P:S], start=True, stop=False)
                pe.matmul(out[:, P:S], V1[:, c, 1, h, :], w[:, S:S + P], start=False,
                          stop=True).then_inc(s_["pv_ready"], 1)

            def back(c, pair):
                pe.wait_ge(s_["vt_ready"], HM // 2 * c + pair + 1)
                if c and pair == 0:
                    pe.wait_ge(s_["taken"], c)
                for t in range(TT):
                    last = pe.transpose(OUTS[:, t, pair * P:pair * P + PAIR], gt[0:PAIR, pair % 2, t * P:(t + 1) * P],
                                        ident[0:PAIR, 0:PAIR])
                last.then_inc(s_["back_ready"], 1)

            def heads_T(c):
                pe.wait_ge(s_["ho_ready"], c + 1)
                if c:
                    pe.wait_ge(s_["x1_ready"], c)
                else:
                    pe.wait_ge(s_["enm_ready"], 1)
                for f in range(KT):
                    for t in range(TT):
                        last = pe.transpose(X[:, f * S + t * P:f * S + (t + 1) * P], ho[:, t, f * P:(f + 1) * P],
                                            ident[:, :])
                last.then_inc(s_["hoT_ready"], 1)

            def project_out(c):
                pe.wait_ge(s_["hoT_split"], c + 1)
                if c == 0:
                    pe.wait_ge(s_["wl_split"], LP)
                for t in range(TT):
                    rows = slice(t * P, (t + 1) * P)
                    last = six(X[:, t * D:(t + 1) * D], [(hTh[:, f, rows], hTl[:, f, rows]) for f in range(KT)],
                               [(WLh[:, 4, f * D:(f + 1) * D], WLl[:, 4, f * D:(f + 1) * D]) for f in range(KT)])
                last.then_inc(s_["wo_ready"], 1)

            def heads(c):
                scores(c, 0)
                for h in range(HM):
                    if h + 1 < HM:
                        scores(c, h + 1)
                    values(c, h)
                    if h == 0 and c:
                        back(c - 1, 3)
                    if h in (2, 4, 6):
                        back(c, h // 2 - 1)
                    if h == AT["T"] and c >= 2:
                        pe_T(pe, 2, c - 2)
                    if h == AT["heads_T"] and c:
                        heads_T(c - 1)
                    if h == AT["out"] and c:
                        project_out(c - 1)

            project(0)
            for c in range(B - 1):
                project_gates(c)
            pe_T(pe, 1, B - 1)
            project_gates(B - 1)
            for c in range(1, B):
                project(c)
            rows_T()
            for c in range(B):
                heads(c)

            def finish_heads(k, c, ht):
                if ht == 0:
                    back(3, 3)
                if ht == 2:
                    pe_T(pe, 2, 2)
                if ht == 4:
                    heads_T(3)
                if ht == 5:
                    project_out(3)
                if ht == 7:
                    pe_T(pe, 2, 3)
            ffn_pe(pe, 1, finish_heads)
            ffn_pe(pe, 2)

        @block.scalar
        def _(act):
            ffn_act(act, 0)
            act.wait_ge(s_["wg_in"], 16)
            act.activation(WGh, wg_f, ACT.Copy).then_inc(s_["wg_hi"], 1)

            def evac(c):
                act.wait_ge(s_["qk_ready"], 2 * c + 1)
                if c:
                    act.wait_ge(s_["qk_split"], 2 * c - 1)
                act.activation(q_hi, UG[0][:, :], ACT.Copy).then_inc(s_["qk_hi"], 1)
                act.wait_ge(s_["qk_ready"], 2 * c + 2)
                act.activation(stack(c, 1), UG[1][:, :], ACT.Copy,
                               scale=cols[:, C_SIGN:C_SIGN + 1]).then_inc(s_["qk_hi"], 1)
                for t in range(TT):
                    act.wait_ge(s_["v_taken"], 2 * c + t + 1)
                    act.activation(og_v[:, c, t, :], UG[2 + t][:, D:2 * D], ACT.Sigmoid).then_inc(s_["og_ready"], 1)

            def gates():
                act.wait_ge(s_["gates_ready"], B)
                act.wait_ge(s_["bgs_ready"], 1)
                for n in range(2):
                    last = act.activation(gt[:, n, :], gate_sums[n], ACT.Tanh, scale=1.0 / CAP,
                                          bias=bgs[:, n:n + 1])
                last.then_inc(s_["gates_tanh"], 1)
                act.wait_ge(s_["gates_tanh"], 1)
                act.activation(gt[:, 1, :], gt[:, 1, :], ACT.Exp, scale=-CAP).then_inc(s_["sp_step"], 1)
                act.wait_ge(s_["sp_step"], 1)
                act.activation(gt[:, 1, :], gt[:, 1, :], ACT.Ln, bias=1.0).then_inc(s_["sp_ready"], 1)

            def exp_nm():
                act.wait_ge(s_["gcol_ready"], 1)
                act.activation(enm[:, :, :], X[:, S:2 * S].rearrange("p (t h) -> p t h", t=TT),
                               ACT.Exp).then_inc(s_["enm_ready"], 1)

            def decay(c, h):
                if h % 4 == 0:
                    act.wait_ge(s_["masked"], 2 * c + h // 4 + 1)
                if c or h >= 2:
                    act.wait_ge(s_["c_ready"], HM * c + h - 1)
                e, a, at = ga[:, h % 2, :], A[c % 2], 32 * c + h
                act.activation(e[:, 0:S], a[:, h, 0:S], ACT.Exp, scale=-1.0, bias=gcol[:, 0, at:at + 1])
                act.activation(e[:, S:S + P], a[:, h, S:S + P], ACT.Exp, scale=-1.0,
                               bias=gcol[:, 1, at:at + 1]).then_inc(s_["e_ready"], 1)

            def take_pair(c, pair):
                act.wait_ge(s_["pv_ready"], HM * c + 2 * pair + 2)
                if c or pair >= 2:
                    act.wait_ge(s_["back_ready"], HM // 2 * c + pair - 1)
                for i in range(2):
                    last = act.activation(gt[64 * i:64 * i + DH + 1, pair % 2, :],
                                          UG[2 + pair % 2][0:DH + 1, i * S:(i + 1) * S], ACT.Copy)
                last.then_inc(s_["vt_ready"], 1)

            def take(c):
                act.wait_ge(s_["back_ready"], HM // 2 * (c + 1))
                if c:
                    act.wait_ge(s_["ho_ready"], c)
                act.activation(hraw_v, heads_v, ACT.Copy).then_inc(s_["taken"], 1)

            def squares(c):
                act.wait_ge(s_["taken"], c + 1)
                if c:
                    act.wait_ge(s_["hoT_ready"], c)
                for t in range(TT):
                    last = act.activation(ho[:, t, :].rearrange("p (h n) -> p h n", h=HM),
                                          hraw_v[:, t, :, 0:DH], ACT.Square)
                last.then_inc(s_["sq_ready"], 1)

            def hoT(c):
                act.wait_ge(s_["hoT_ready"], c + 1)
                if c:
                    act.wait_ge(s_["wo_ready"], c)
                for f in range(KT):
                    last = act.activation(hTh[:, f, :], X[:, f * S:(f + 1) * S], ACT.Copy,
                                          scale=cols[:, C_MH + f:C_MH + f + 1])
                last.then_inc(s_["hoT_hi"], 1)

            def mlp_hi(lo_, hi_):
                for i in range(lo_, hi_):
                    act.wait_ge(wm_in[i % RING], 16 * (i // RING + 1))
                    if i == 0:
                        act.wait_ge(ffn_sems[0]["down"], FT * B)
                    act.activation(mlp_place(i, True), raw[:, i % RING, :], ACT.Copy).then_inc(s_["wm_hi"], 1)

            act_ssq(act, 1, 3)
            evac(0)
            act_hi(act, 1, 3)
            mlp_hi(0, 2)
            gates()
            evac(1)
            mlp_hi(2, 4)
            evac(2)
            mlp_hi(4, 5)
            evac(3)
            exp_nm()
            for c in range(B):
                for h in range(HM):
                    decay(c, h)
                    if h == 0 and c:
                        take_pair(c - 1, 3)
                    if h in (3, 5, 7):
                        take_pair(c, (h - 3) // 2)
                    if h == AT["take"] and c:
                        take(c - 1)
                    if h == AT["squares"] and c:
                        squares(c - 1)
                    if h == AT["ssq"] and c >= 2:
                        act_ssq(act, 2, c - 2)
                    if h == AT["hi"] and c >= 2:
                        act_hi(act, 2, c - 2)
                    if h == AT["hoT_hi"] and c:
                        hoT(c - 1)
                    if c < 3 and h >= 8 - MLP_PIECES[c]:
                        i = 5 + sum(MLP_PIECES[:c]) + h - 8 + MLP_PIECES[c]
                        mlp_hi(i, i + 1)
            take_pair(3, 3)

            def finish_heads(k, c, ht):
                if ht == 0:
                    take(3)
                    squares(3)
                    act_ssq(act, 2, 2)
                if ht == 2:
                    act_hi(act, 2, 2)
                if ht == 4:
                    hoT(3)
                if ht == 5:
                    act_ssq(act, 2, 3)
                if ht == 7:
                    act_hi(act, 2, 3)
            ffn_act(act, 1, finish_heads)
            ffn_act(act, 2)

        @block.vector
        def _(dve):
            dve.memset(ones[:, :], 1.0).then_inc(s_["consts_set"], 1)
            dve.memset(mhalf[:, :], -0.5).then_inc(s_["consts_set"], 1)
            dve.memset(V1[:, :, :, :, DH:DH + 1], 1.0).then_inc(s_["consts_set"], 1)
            ffn_dve(dve, 0)
            dve.wait_ge(s_["wg_hi"], 1)
            dve.tensor_tensor(WGl, wg_f, WGh.bitcast(F32), ALU.subtract).then_inc(s_["wg_split"], 1)
            dve.wait_ge(s_["small_in"], 64)
            dve.tensor_scalar(bgs[:, :], bg[:, :], 1.0 / CAP, None, ALU.mult).then_inc(s_["bgs_ready"], 1)

            def chain():
                dve.wait_ge(s_["sp_ready"], 1)
                dve.wait_ge(s_["consts_set"], 3)
                dve.tensor_tensor_scan(cumS[:, :], ones[:, :], gt[:, 1, :], 0.0, ALU.mult, ALU.add).then_inc(s_["cs_ready"], 1)
                dve.wait_ge(s_["cs_ready"], 1)
                dve.scalar_tensor_tensor(gr[:, :], gt[:, 0, :], CAP, cumS[:, :], ALU.mult, ALU.add).then_inc(s_["gr_ready"], 1)
                dve.wait_ge(s_["gr_ready"], 1)
                dve.tensor_tensor_scan(M[:, :], ones[:, :], gr[:, :], -BIG, ALU.mult, ALU.max).then_inc(s_["m_ready"], 1)
                dve.wait_ge(s_["m_ready"], 1)
                dve.tensor_tensor(nm[:, :], cumS[:, :], M[:, :], ALU.subtract).then_inc(s_["nm_ready"], 1)

            def split(c):
                dve.wait_ge(s_["qk_hi"], 2 * c + 1)
                dve.scalar_tensor_tensor(stack(c, 0), UG[0][:, :], cols[:, C_LO:C_LO + 1], q_hi.bitcast(F32),
                                         ALU.mult, ALU.subtract).then_inc(s_["qk_split"], 1)
                dve.wait_ge(s_["qk_hi"], 2 * c + 2)
                dve.scalar_tensor_tensor(stack(c, 2), UG[1][:, :], cols[:, C_SIGN:C_SIGN + 1],
                                         stack(c, 1).bitcast(F32), ALU.mult, ALU.subtract).then_inc(s_["qk_split"], 1)
                for t in range(TT):
                    dve.wait_ge(s_["vog_ready"], 2 * c + t + 1)
                    dve.tensor_copy(V1[:, c, t, :, 0:DH], UG[2 + t][:, 0:D].rearrange("p (h n) -> p h n", h=HM))\
                        .then_inc(s_["v_taken"], 1)

            def weigh(c, h):
                dve.wait_ge(s_["st_ready"], HM * c + h + 1)
                dve.wait_ge(s_["e_ready"], HM * c + h + 1)
                if c or h >= 2:
                    dve.wait_ge(s_["pv_ready"], HM * c + h - 1)
                dve.scalar_tensor_tensor(gb[:, h % 2, :], UG[h % 2][:, 0:384], 1.0 / math.sqrt(DQ), ga[:, h % 2, :],
                                         ALU.mult, ALU.mult).then_inc(s_["c_ready"], 1)

            def norm_a(c):
                nn_v, sums = nn[:, :].rearrange("p (t h) -> p t h", t=TT), hraw_v[:, :, :, DH]
                dve.wait_ge(s_["taken"], c + 1)
                if c == 0:
                    dve.wait_ge(s_["enm_ready"], 1)
                dve.scalar_tensor_tensor(nn_v, sums, -1.0, enm[:, :, 32 * c:32 * c + HM], ALU.mult,
                                         ALU.max).then_inc(s_["abs_ready"], 1)
                dve.wait_ge(s_["abs_ready"], c + 1)
                dve.scalar_tensor_tensor(nn_v, sums, 1.0, nn_v, ALU.mult, ALU.max).then_inc(s_["nn_ready"], 1)
                dve.wait_ge(s_["nn_ready"], c + 1)
                dve.scalar_tensor_tensor(n2[:, :], nn[:, :], RMS_EPS, nn[:, :], ALU.mult, ALU.mult).then_inc(s_["n2_ready"], 1)
                dve.wait_ge(s_["sq_ready"], c + 1)
                dve.tensor_reduce(msq[:, :].rearrange("p (t h) -> p t h", t=TT),
                                  ho[:, :, :].rearrange("p t (h n) -> p t h n", h=HM), axis=AX.X,
                                  op=ALU.add).then_inc(s_["sum_ready"], 1)
                dve.wait_ge(s_["sum_ready"], c + 1)
                dve.wait_ge(s_["n2_ready"], c + 1)
                dve.scalar_tensor_tensor(hv[:, :], msq[:, :], 1.0 / DH, n2[:, :], ALU.mult, ALU.add).then_inc(s_["msq_ready"], 1)

            def norm_b(c):
                dve.wait_ge(s_["hsc_ready"], c + 1)
                for t in range(TT):
                    sc = hsc[:, t * HM:(t + 1) * HM].rearrange("p (h n) -> p h n", n=1).broadcast_to([P, HM, DH])
                    last = dve.tensor_tensor(ho[:, t, :].rearrange("p (h n) -> p h n", h=HM), hraw_v[:, t, :, 0:DH], sc,
                                             ALU.mult)
                last.then_inc(s_["hs_ready"], 1)
                dve.wait_ge(s_["hs_ready"], c + 1)
                dve.wait_ge(s_["og_ready"], 2 * c + 2)
                dve.tensor_tensor(ho[:, :, :], ho[:, :, :], og_v[:, c, :, :], ALU.mult).then_inc(s_["ho_ready"], 1)

            def hoT(c):
                dve.wait_ge(s_["hoT_hi"], c + 1)
                for f in range(KT):
                    last = dve.scalar_tensor_tensor(hTl[:, f, :], X[:, f * S:(f + 1) * S], cols[:, C_MH + f:C_MH + f + 1],
                                                    hTh[:, f, :].bitcast(F32), ALU.mult, ALU.subtract)
                last.then_inc(s_["hoT_split"], 1)

            def add_heads(c):
                dve.wait_ge(s_["wo_ready"], c + 1)
                dve.tensor_tensor(x1_v[:, c, :, :], X[:, :].rearrange("p (t d) -> p t d", t=TT), res_v[:, c, :, :],
                                  ALU.add).then_inc(s_["x1_ready"], 1)
                dve.wait_ge(s_["x1_ready"], c + 1)
                dve.tensor_tensor(res_v[:, c, :, :], x1_v[:, c, :, :], res_v[:, c, :, :], ALU.add).then_inc(s_["x1_mid"], 1)

            add_out(dve, 0, 3)
            dve_stats(dve, 1, 3)
            dve_apply(dve, 1, 3)
            split(0)
            dve_xs(dve, 1, 3)
            dve_lo(dve, 1, 3)
            chain()
            split(1)
            split(2)
            split(3)
            dve.wait_ge(s_["rows_ready"], 1)
            dve.tensor_copy(gcol[:, :, :], X[:, 0:S].rearrange("p (t h) -> p t h", t=TT)).then_inc(s_["gcol_ready"], 1)
            for c in range(B):
                for h in range(HM):
                    weigh(c, h)
                    if h == AT["norm_a"] and c:
                        norm_a(c - 1)
                    if h == AT["xs"] and c >= 2:
                        dve_xs(dve, 2, c - 2)
                    if h == AT["hi"] and c >= 2:
                        dve_lo(dve, 2, c - 2)
                    if h == AT["norm_b"] and c:
                        norm_b(c - 1)
                    if h == AT["hoT_lo"] and c:
                        hoT(c - 1)
                if c:
                    add_heads(c - 1)

            def finish_heads(k, c, ht):
                if ht == 0:
                    norm_a(3)
                if ht == 1:
                    dve_xs(dve, 2, 2)
                if ht == 2:
                    dve_lo(dve, 2, 2)
                if ht == 3:
                    norm_b(3)
                if ht == 4:
                    hoT(3)
                if ht == 5:
                    add_heads(3)
                if ht == 6:
                    dve_xs(dve, 2, 3)
                if ht == 7:
                    dve_lo(dve, 2, 3)
            ffn_dve(dve, 1, finish_heads)
            ffn_dve(dve, 2)
            add_out(dve, 2, 3)
            dve_stats(dve, 4, 3)
            dve_apply(dve, 4, 3)

        @block.gpsimd
        def _(pool):
            pool.wait_ge(s_["consts_set"], 3)
            def int8_pieces(c):
                pool.wait_ge(s_["st_ready"], HM * B)
                pool.wait_ge(s_["int8_in"], 16)
                for i in range(4):
                    pool.tensor_copy(WI[:, (c - 1) * 4 + i, :], raw8[:, (c - 1) * 4 + i, :]).then_inc(s_["int8_done"], 1)
            pool_ln(pool, 0, B - 1)
            pool.wait_ge(s_["wl_in"], 16)
            def split_wl(i):
                pool.tensor_copy(WLh[:, i, :], raw[:, i, :]).then_inc(s_["wl_hi"], 1)
                pool.wait_ge(s_["wl_hi"], i + 1)
                pool.tensor_tensor(WLl[:, i, :], raw[:, i, :], WLh[:, i, :].bitcast(F32), ALU.subtract).then_inc(s_["wl_split"], 1)
            for i in range(LP - 1):
                split_wl(i)
            ffn_pool(pool, 0)
            split_wl(LP - 1)
            pool_ln(pool, 1, 3)
            pool_rms(pool, 1, 3)

            def add_mask(c):
                pool.wait_ge(a_in[c % 2], 32 * (c // 2 + 1))
                for half in range(2):
                    a = A[c % 2][:, 4 * half:4 * half + 4, :].rearrange("p h (b n) -> p h b n", n=P)[:, :, 0:3:2, :]
                    m = mask[:, :].rearrange("p (a b n) -> p a b n", a=1, b=1).broadcast_to([P, 4, 2, P])
                    pool.tensor_tensor(a, a, m, ALU.add).then_inc(s_["masked"], 1)

            def head_scales(c):
                pool.wait_ge(s_["msq_ready"], c + 1)
                if c:
                    pool.wait_ge(s_["hs_ready"], c)
                pool.tensor_tensor(hsc[:, :], hv[:, :], mhalf[:, :], ALU.pow).then_inc(s_["hsc_ready"], 1)

            def split_mlp(lo_, hi_):
                for i in range(lo_, hi_):
                    pool.wait_ge(s_["wm_hi"], i + 1)
                    pool.tensor_tensor(mlp_place(i, False), raw[:, i % RING, :], mlp_place(i, True).bitcast(F32),
                                       ALU.subtract).then_inc(s_["wm_split"], 1)

            split_mlp(0, 5)
            add_mask(0)
            add_mask(1)
            split_mlp(5, 8)
            head_scales(0)
            add_mask(2)
            split_mlp(8, 10)
            pool_rms(pool, 2, 0)
            head_scales(1)
            add_mask(3)
            split_mlp(10, 12)
            pool_rms(pool, 2, 1)
            head_scales(2)
            pool_rms(pool, 2, 2)
            head_scales(3)
            ffn_pool(pool, 1, int8_pieces)
            ffn_pool(pool, 2)
            pool_ln(pool, 4, 3)


def _layout(i):
    f = np.float32
    x = i["L0_attn_hidden_states"].reshape(TOK, D)

    def by_kt(m):
        return m.reshape(-1, P, m.shape[1]).transpose(1, 0, 2)

    Wq, Wk, Wv, Wo = (i["L0_attn_" + n] for n in ("Wq", "Wk", "Wv", "Wo"))
    w_att = np.empty((NG, P, GP, PIECE), f)
    for g in range(NG):
        rot = [W[H * DN:].reshape(H, 2, DR // 2, D)[HG * g:HG * g + HG, half].reshape(P, D)
               for W in (Wq, Wk) for half in range(2)]
        w_att[g, :, 0:2] = by_kt(np.concatenate(rot).T)
        for pair in range(2):
            h = HG * g + 2 * pair
            w_att[g, :, 2 + 2 * pair:4 + 2 * pair] = by_kt(
                np.concatenate([W[n * DN:(n + 1) * DN] for n in (h, h + 1) for W in (Wq, Wk)]).T)
        w_att[g, :, 6:8] = by_kt(Wv[g * PIECE:(g + 1) * PIECE].T)
        w_att[g, :, 8:10] = Wo[:, g * PIECE:(g + 1) * PIECE].T.reshape(2, 2, P, D).transpose(2, 0, 1, 3).reshape(P, 2, PIECE)

    def gate_up(gate, up):
        both = np.stack([gate.reshape(D, FT, P), up.reshape(D, FT, P)], 2)
        return both.reshape(KT, P, 4, PIECE).transpose(1, 0, 2, 3).reshape(P, 8, PIECE)

    def down(m):
        return by_kt(m).reshape(P, 4, PIECE)

    def heads(m):
        return np.repeat(m.reshape(D, HM, 1, DQ), 2, 2).reshape(D, 2 * P)

    def pad(a, before, n):
        return np.concatenate([np.zeros(a.shape[:-1] + (before,), f), a,
                               np.zeros(a.shape[:-1] + (n - before - a.shape[-1],), f)], -1)

    L1 = {n[8:]: v for n, v in i.items() if n.startswith("L1_attn_")}
    F1 = {n[7:]: v for n, v in i.items() if n.startswith("L1_ffn_")}
    wl = np.empty((P, LP, PIECE), f)
    wl[:, 0:2] = by_kt(np.concatenate([heads(L1["wq"]), heads(L1["wk"])], 1))
    wl[:, 2:4] = by_kt(np.concatenate([L1["wv"], L1["w_og"]], 1))
    wl[:, 4] = by_kt(L1["w_out"]).reshape(P, PIECE)

    t = np.arange(S, dtype=f)[:, None]
    inv = (f(1.0) / f(10000.0) ** (np.arange(0, DR, 2, dtype=f) / f(DR))).astype(f)
    angle = (t * inv).astype(f)
    tab = np.tile(np.stack([np.cos(angle).T, np.sin(angle).T]), (1, HG, 1)).transpose(1, 0, 2)
    rope = np.stack([tab * f(math.sqrt(DN / DR)), tab], 1).astype(f)
    lower = (np.arange(P)[:, None] % 32 >= DQ).astype(f)
    had = np.ones((1, 1), f)
    while len(had) < P:
        had = np.block([[had, had], [had, -had]])
    return {
        "x_tok": x, "x_T": x.T, "w_att": w_att,
        "w_ffn0": gate_up(i["L0_ffn_W1"].T, i["L0_ffn_W3"].T), "w2_raw": down(i["L0_ffn_W2"].T),
        "rope": rope, "ident_d": np.eye(P, dtype=f), "had_d": had * f(1 / math.sqrt(FF)),
        "wl_d": wl, "wg_d": by_kt(np.concatenate([pad(L1["w_ig"], 96, WIDE), pad(L1["w_fg"], 96, WIDE)], 1)).reshape(P, -1),
        "bg_d": np.tile(pad(np.stack([L1["b_ig"], L1["b_fg"]]), 0, 32).T, (B, 1)),
        "cols_d": np.concatenate([v.reshape(-1, P).T for v in (L1["norm1_w"], L1["mh_w"], L1["norm2_w"], F1["s_gate"], F1["s_up"])]
                                 + [lower, 2 * lower - 1], 1),
        "mask_d": np.tril(np.full((P, P), BIG, f), -1),
        "wm_d": np.concatenate([gate_up(L1["w_gate"], L1["w_up"]), down(L1["w_down"])], 1),
        "w8_d": np.ascontiguousarray(
            np.concatenate([gate_up(F1["w_gate"], F1["w_up"]), down(F1["w_down"])], 1).reshape(P, 12 * PIECE)).view(np.int32),
        "sdown_d": F1["s_down"].reshape(1, D),
    }


def build(nc, out_d, x_tok, x_T, w_att, w_ffn0, w2_raw, rope, ident_d, had_d, **later):
    with ExitStack() as ctx:
        def sb(name, shape, dt):
            return ctx.enter_context(nc.sbuf_tensor(name, shape, dt))

        keep = {
            "xTh": sb("xTh", [P, KT, TOK], F32R), "xTl": sb("xTl", [P, KT, TOK], F32R),
            "WBh": sb("WBh", [P, FT, PIECE], F32R), "WBl": sb("WBl", [P, FT, PIECE], F32R),
            "xres": sb("xres", [P, B * TT, D], F32), "ident": sb("ident", [P, P], F32),
            "QKh": sb("QKh", [P, 2, HG, 2 * S], F32R), "QKl": sb("QKl", [P, 2, HG, 2 * S], F32R),
            "stage": sb("stage", [P, HM * 384], F32),
        }
        attention(nc, keep, x_tok, x_T, w_att, w_ffn0, w2_raw, rope, ident_d, had_d)
        layers(nc, keep, out_d=out_d, **later)


def kernel(**inputs):
    import concourse.bacc as bacc
    from concourse.bass_utils import run_bass_kernel_spmd

    nc = bacc.Bacc("TRN2", target_bir_lowering=False, num_devices=1)
    arrays = {n: np.ascontiguousarray(a) for n, a in _layout({n: np.asarray(a) for n, a in inputs.items()}).items()}
    args = {n: nc.dram_tensor("in_" + n, a.shape, mybir.dt.from_np(a.dtype), kind="ExternalInput").ap()
            for n, a in arrays.items()}
    out = nc.dram_tensor("out_x", (TOK, D), F32, kind="ExternalOutput").ap()
    build(nc, out, **args)
    r = run_bass_kernel_spmd(nc, [{"in_" + n: a for n, a in arrays.items()}], core_ids=[0])
    return r.results[0]["out_x"].reshape(B, S, D)
```
